# Optimizing a Trainium2 kernel written in Bass

```python
import numpy as np
import jax
import jax.numpy as jnp

def _softmax(x, axis=-1):
    return jax.nn.softmax(x, axis=axis)
def _gelu(x):
    return jax.nn.gelu(x, approximate=True)
def _silu(x):
    return jax.nn.silu(x)
def _sigmoid(x):
    return jax.nn.sigmoid(x)
def _layernorm(x, axis=-1, eps=1e-5):
    m = jnp.mean(x, axis=axis, keepdims=True)
    v = jnp.var(x, axis=axis, keepdims=True)
    return (x - m) / jnp.sqrt(v + eps)
def _scatter_add(tgt, idx, src, axis=0):
    return tgt.at[idx].add(src)
def _segment_sum(src, seg, n):
    return jax.ops.segment_sum(src, seg, n)

kernel_name = 'mk_conv_preact_d2_conv_nhwc128_db3f7d'

def setup_inputs(seed: int = 0):
    np.random.seed(seed)
    _w = jnp.asarray
    def _rec_inputs():
        import jax
        import jax.numpy as jnp
        _gk = jax.random.key(seed)
        x = -0.0002091 + 1 * jax.random.normal(jax.random.fold_in(_gk, 1), (64, 56, 56, 128), jnp.float32)
        return x
    x = _rec_inputs()
    def _L0_conv_setup():
        import jax, jax.numpy as jnp
        import numpy as np
        DIM = 128
        NUM_HEADS = 4
        WS = 7
        SHIFT = 3
        H = W = 56
        B = 64
        SCALE = DIM ** (-0.5)
        NEG_INF = -1000000000.0

        def _make_attn_mask():
            img = np.zeros((H, W), dtype=np.float32)
            slices = (slice(0, -WS), slice(-WS, -SHIFT), slice(-SHIFT, None))
            cnt = 0
            for hs in slices:
                for ws_ in slices:
                    img[hs, ws_] = cnt
                    cnt += 1
            m = img.reshape(H // WS, WS, W // WS, WS).transpose(0, 2, 1, 3).reshape(-1, WS * WS)
            am = m[:, None, :] - m[:, :, None]
            am = np.where(am != 0, NEG_INF, 0.0).astype(np.float32)
            return jnp.asarray(am)

        def _window_partition(x):
            Bx, Hx, Wx, C = x.shape
            x = x.reshape(Bx, Hx // WS, WS, Wx // WS, WS, C)
            x = x.transpose(0, 1, 3, 2, 4, 5)
            return x.reshape(-1, WS * WS, C)

        def _window_reverse(w):
            C = w.shape[-1]
            x = w.reshape(B, H // WS, W // WS, WS, WS, C)
            x = x.transpose(0, 1, 3, 2, 4, 5)
            return x.reshape(B, H, W, C)
        key = jax.random.key(seed)
        k1, k2, k3 = jax.random.split(key, 3)
        x = jax.random.normal(k1, (B, H, W, DIM), dtype=jnp.float32)
        qkv_w = jax.random.normal(k2, (DIM, 3 * DIM), dtype=jnp.float32) * 0.02
        qkv_b = jnp.zeros((3 * DIM,), dtype=jnp.float32)
        proj_w = jax.random.normal(k3, (DIM, DIM), dtype=jnp.float32) * 0.02
        proj_b = jnp.zeros((DIM,), dtype=jnp.float32)
        return {'x': x, 'qkv_w': qkv_w, 'qkv_b': qkv_b, 'proj_w': proj_w, 'proj_b': proj_b}
    _L0_conv_all = _L0_conv_setup()
    _L0_conv_in = {k: v for k, v in _L0_conv_all.items() if k in ('qkv_w', 'qkv_b', 'proj_w', 'proj_b', )}
    del _L0_conv_all

    def _L1_conv_setup():
        import jax, jax.numpy as jnp
        import numpy as np
        WS = 7
        NH = 4

        def _relative_position_index(ws: int) -> np.ndarray:
            coords = np.stack(np.meshgrid(np.arange(ws), np.arange(ws), indexing='ij'))
            coords = coords.reshape(2, -1)
            rel = coords[:, :, None] - coords[:, None, :]
            rel = rel.transpose(1, 2, 0) + (ws - 1)
            rel[:, :, 0] *= 2 * ws - 1
            return rel.sum(-1)
        REL_IDX = _relative_position_index(WS)
        key = jax.random.key(seed)
        k1, k2, k3, k4 = jax.random.split(key, 4)
        dim = 128
        x = jax.random.normal(k1, (64, 56, 56, dim), dtype=jnp.float32)
        qkv_w = jax.random.normal(k2, (dim, 3 * dim), dtype=jnp.float32) * dim ** (-0.5)
        qkv_b = jnp.zeros((3 * dim,), dtype=jnp.float32)
        proj_w = jax.random.normal(k3, (dim, dim), dtype=jnp.float32) * dim ** (-0.5)
        proj_b = jnp.zeros((dim,), dtype=jnp.float32)
        bias_table = jax.random.truncated_normal(k4, -2.0, 2.0, ((2 * WS - 1) ** 2, NH), dtype=jnp.float32) * 0.02
        return {'x': x, 'qkv_w': qkv_w, 'qkv_b': qkv_b, 'proj_w': proj_w, 'proj_b': proj_b, 'bias_table': bias_table}
    _L1_conv_all = _L1_conv_setup()
    _L1_conv_in = {k: v for k, v in _L1_conv_all.items() if k in ('qkv_w', 'qkv_b', 'proj_w', 'proj_b', 'bias_table', )}
    del _L1_conv_all

    return {
        "x": x,
        "L0_conv_qkv_w": _L0_conv_in["qkv_w"],
        "L0_conv_qkv_b": _L0_conv_in["qkv_b"],
        "L0_conv_proj_w": _L0_conv_in["proj_w"],
        "L0_conv_proj_b": _L0_conv_in["proj_b"],
        "L1_conv_qkv_w": _L1_conv_in["qkv_w"],
        "L1_conv_qkv_b": _L1_conv_in["qkv_b"],
        "L1_conv_proj_w": _L1_conv_in["proj_w"],
        "L1_conv_proj_b": _L1_conv_in["proj_b"],
        "L1_conv_bias_table": _L1_conv_in["bias_table"],
    }

def reference(x, L0_conv_qkv_w, L0_conv_qkv_b, L0_conv_proj_w, L0_conv_proj_b, L1_conv_qkv_w, L1_conv_qkv_b, L1_conv_proj_w, L1_conv_proj_b, L1_conv_bias_table):
    import jax
    import jax.numpy as jnp
    def _L0_conv_ref(x, qkv_w, qkv_b, proj_w, proj_b):
        import jax, jax.numpy as jnp
        import numpy as np
        DIM = 128
        NUM_HEADS = 4
        WS = 7
        SHIFT = 3
        H = W = 56
        B = 64
        SCALE = DIM ** (-0.5)
        NEG_INF = -1000000000.0

        def _make_attn_mask():
            img = np.zeros((H, W), dtype=np.float32)
            slices = (slice(0, -WS), slice(-WS, -SHIFT), slice(-SHIFT, None))
            cnt = 0
            for hs in slices:
                for ws_ in slices:
                    img[hs, ws_] = cnt
                    cnt += 1
            m = img.reshape(H // WS, WS, W // WS, WS).transpose(0, 2, 1, 3).reshape(-1, WS * WS)
            am = m[:, None, :] - m[:, :, None]
            am = np.where(am != 0, NEG_INF, 0.0).astype(np.float32)
            return jnp.asarray(am)

        def _window_partition(x):
            Bx, Hx, Wx, C = x.shape
            x = x.reshape(Bx, Hx // WS, WS, Wx // WS, WS, C)
            x = x.transpose(0, 1, 3, 2, 4, 5)
            return x.reshape(-1, WS * WS, C)

        def _window_reverse(w):
            C = w.shape[-1]
            x = w.reshape(B, H // WS, W // WS, WS, WS, C)
            x = x.transpose(0, 1, 3, 2, 4, 5)
            return x.reshape(B, H, W, C)
        attn_mask = _make_attn_mask()
        N = WS * WS
        hd = DIM // NUM_HEADS
        shifted = jnp.roll(x, shift=(-SHIFT, -SHIFT), axis=(1, 2))
        xw = _window_partition(shifted)
        qkv = xw @ qkv_w + qkv_b
        qkv = qkv.reshape(-1, N, 3, NUM_HEADS, hd)
        q, k, v = (qkv[:, :, 0], qkv[:, :, 1], qkv[:, :, 2])
        attn = jnp.einsum('wnhd,wmhd->whnm', q, k) * SCALE
        nW = attn_mask.shape[0]
        attn = attn.reshape(B, nW, NUM_HEADS, N, N) + attn_mask[None, :, None, :, :]
        attn = jax.nn.softmax(attn.reshape(-1, NUM_HEADS, N, N), axis=-1)
        out = jnp.einsum('whnm,wmhd->wnhd', attn, v).reshape(-1, N, DIM)
        out = out @ proj_w + proj_b
        shifted_out = _window_reverse(out)
        return jnp.roll(shifted_out, shift=(SHIFT, SHIFT), axis=(1, 2))

    def _L1_conv_ref(x, qkv_w, qkv_b, proj_w, proj_b, bias_table):
        import jax, jax.numpy as jnp
        import numpy as np
        WS = 7
        NH = 4

        def _relative_position_index(ws: int) -> np.ndarray:
            coords = np.stack(np.meshgrid(np.arange(ws), np.arange(ws), indexing='ij'))
            coords = coords.reshape(2, -1)
            rel = coords[:, :, None] - coords[:, None, :]
            rel = rel.transpose(1, 2, 0) + (ws - 1)
            rel[:, :, 0] *= 2 * ws - 1
            return rel.sum(-1)
        REL_IDX = _relative_position_index(WS)
        B, H, W, C = x.shape
        ws, nh = (WS, NH)
        hd = C // nh
        N = ws * ws
        xw = x.reshape(B, H // ws, ws, W // ws, ws, C).transpose(0, 1, 3, 2, 4, 5).reshape(-1, N, C)
        qkv = xw @ qkv_w + qkv_b
        qkv = qkv.reshape(-1, N, 3, nh, hd).transpose(2, 0, 3, 1, 4)
        q, k, v = (qkv[0], qkv[1], qkv[2])
        attn = jnp.einsum('whqd,whkd->whqk', q, k) * hd ** (-0.5)
        rel_bias = bias_table[REL_IDX.reshape(-1)].reshape(N, N, nh).transpose(2, 0, 1)
        attn = jax.nn.softmax(attn + rel_bias[None], axis=-1)
        out = jnp.einsum('whqk,whkd->whqd', attn, v)
        out = out.transpose(0, 2, 1, 3).reshape(-1, N, C)
        out = out @ proj_w + proj_b
        out = out.reshape(B, H // ws, W // ws, ws, ws, C).transpose(0, 1, 3, 2, 4, 5).reshape(B, H, W, C)
        return out

    def _gn(v, G=32, eps=1e-5):
        B_, H_, W_, C_ = v.shape
        g = v.reshape(B_, H_, W_, G, C_ // G)
        m = jnp.mean(g, axis=(1, 2, 4), keepdims=True)
        s = jnp.var(g, axis=(1, 2, 4), keepdims=True)
        return ((g - m) / jnp.sqrt(s + eps)).reshape(v.shape)

    def _ln_c(v, eps=1e-6):
        m = jnp.mean(v, axis=-1, keepdims=True)
        s = jnp.var(v, axis=-1, keepdims=True)
        return (v - m) / jnp.sqrt(s + eps)

    def _ln_t(v, eps=1e-5):
        m = jnp.mean(v, axis=-1, keepdims=True)
        s = jnp.var(v, axis=-1, keepdims=True)
        return (v - m) / jnp.sqrt(s + eps)

    def _to_tokens(v):
        B_, H_, W_, C_ = v.shape
        return v.reshape(B_, H_ * W_, C_)
    def _from_tokens(t, like):
        return t.reshape(like.shape)

    x = x + _L0_conv_ref(_gn(x), L0_conv_qkv_w, L0_conv_qkv_b, L0_conv_proj_w, L0_conv_proj_b)
    x = x + _L1_conv_ref(_gn(x), L1_conv_qkv_w, L1_conv_qkv_b, L1_conv_proj_w, L1_conv_proj_b, L1_conv_bias_table)
    return x


_drawn_inputs = setup_inputs


def setup_inputs(seed=0):
    import zlib

    import numpy as np

    out = dict(_drawn_inputs(seed))
    spreads = {'L0_conv_qkv_b': (0.0, 0.269),
     'L0_conv_proj_b': (0.0, 0.1),
     'L1_conv_qkv_b': (0.0, 0.1),
     'L1_conv_proj_b': (0.0, 0.1)}
    factors = {'L0_conv_qkv_w': 6.21, 'L1_conv_bias_table': 8.0}
    for name, (base, spread) in spreads.items():
        noise = np.random.default_rng([zlib.crc32(name.encode()), seed]).standard_normal(out[name].shape)
        drawn = base * np.exp(spread * noise) if base else spread * noise
        out[name] = jnp.asarray(drawn.astype(out[name].dtype))
    for name, factor in factors.items():
        out[name] = (out[name] * factor).astype(out[name].dtype)
    return out
```

```python
from contextlib import ExitStack

import concourse.bass as bass
from concourse import mybir

F32 = mybir.dt.float32
ACT = mybir.ActivationFunctionType
ALU = mybir.AluOpType
AX = mybir.AxisListType

IMAGES, SIDE, CH = 64, 56, 128
WS, SHIFT, HEADS, GROUPS = 7, 3, 4, 32
HD = CH // HEADS
N = WS * WS
WPAD = 64
WINS = SIDE // WS
PAIRS = WINS // 2
STRIPS = SIDE // WS
TOK = WINS * N
PITCH = SIDE + SHIFT
ROWS_STRIP = WS * PITCH
IMG = PITCH * PITCH
RING = 3
TOTAL = IMAGES * STRIPS
LAG = 2 * STRIPS
LEAD = 2 * STRIPS
JT = 4
PT = TOK // JT
VW = HD + 1
GN_EPS = 1e-5
TABLE_SIDE = 2 * WS - 1
SCALE = {"A": float(CH) ** -0.5, "B": float(HD) ** -0.5}

STEPS = 2 * TOTAL
ALONE = LAG
SCHEDULE = [(-2, 2, False), (2, ALONE - 2, True), (ALONE - 2, ALONE + 4, False),
            (ALONE + 4, STEPS - ALONE - 2, True), (STEPS - ALONE - 2, STEPS - ALONE + 2, False),
            (STEPS - ALONE + 2, STEPS - 2, True), (STEPS - 2, STEPS + 2, False)]


def place(win):
    pp, w, a = win // 4, win // 2 % 2, win % 2
    return 2 * pp + a, w


class Step:

    def __init__(self, n, stream, strip, parity, part):
        self.n, self.stream, self.strip = n, stream, strip
        self.parity = parity
        self.part = part
        self.g = strip if stream == "A" else strip + LAG
        self.leads = stream == "A" or part == 2


def step_at(u):
    if u < 0 or u >= STEPS:
        return None
    if u < ALONE:
        return Step(u, "A", u, u % 2, 0)
    if u >= STEPS - ALONE:
        return Step(u, "B", u - TOTAL, u % 2, 2)
    if u % 2 == 0:
        return Step(u, "A", LAG + (u - ALONE) // 2, 0, 1)
    return Step(u, "B", (u - ALONE) // 2, 1, 1)


def later(step, it):
    rate = 1 if step.part == 1 else 2
    return Step(step.n + it * 2, step.stream, step.strip + it * rate, step.parity, step.part)


def walk(eng, body):
    for lo, hi, looped in SCHEDULE:
        if looped:
            with eng.Fori(0, (hi - lo) // 2) as it:
                for u in (lo, lo + 1):
                    body(*[later(step_at(u + k), it) for k in (-2, -1, 0, 1, 2)])
        else:
            for u in range(lo, hi):
                body(*[step_at(u + k) for k in (-2, -1, 0, 1, 2)])


def at_least(eng, sem, value):
    if not isinstance(value, int) or value > 0:
        eng.wait_ge(sem, value)


def when(eng, value, wanted, body):
    if isinstance(value, int):
        if value == wanted:
            body()
    else:
        with eng.If(value == wanted):
            body()


def ring_at(eng, strip):
    r = strip % (RING * STRIPS)
    gap = IMG - STRIPS * ROWS_STRIP
    if isinstance(strip, int):
        return r * ROWS_STRIP + (r // STRIPS) * gap
    r = eng.snap(r)
    return eng.snap(r * ROWS_STRIP + (r >> 3) * gap).with_bounds(min_val=0, max_val=RING * IMG - gap - ROWS_STRIP)


def rows(ring, off, col, width=SIDE, n=WS):
    v = ring[:, bass.ds(off + col, (n - 1) * PITCH + width)]
    return bass.AP(v.tensor, v.offset, [v.ap[0], [PITCH, n], [1, width]])


X_MEAN, X_VAR = 0, 1
X1_CHAN, X1_MEAN, X1_VAR = 0, 3, 5


def at_time(eng, step, phase, body):
    if step is None or not step.leads:
        return
    if isinstance(step.g, int):
        if STRIPS <= step.g < TOTAL + STRIPS:
            when(eng, step.g % STRIPS, phase, body)
    elif step.part == 1:
        when(eng, step.g & (STRIPS - 1), phase, body)
    else:
        when(eng, step.g, phase + (STRIPS if step.part == 0 else TOTAL), body)


def window_attention_layers(nc, x, qkv_w, qkv_b, proj_w, proj_b, bias_rev, mask, ident_in, group_in, out):
    with ExitStack() as ctx:
        ctx.enter_context(nc.allow_non_contiguous_dma("small loads of biases and the relative bias table"))

        def sb(name, shape):
            return ctx.enter_context(nc.sbuf_tensor(name, shape, F32))

        def sem(name):
            return ctx.enter_context(nc.semaphore(name))

        score_banks = ctx.enter_context(nc.psum_tensor("score_banks", [128, HEADS, 512], F32))
        q_bank, k_bank, v_bank, ot_bank = [
            ctx.enter_context(nc.psum_tensor(f"{b}_bank", [128, 512], F32)) for b in ("q", "k", "v", "ot")]
        y_bank = k_bank
        o_banks = [v_bank, ot_bank]
        swap_bank = score_banks[:, 2, :]
        stat_col = swap_bank[:, 508:509]

        ident = sb("ident", [128, 128])
        group_avg = sb("group_avg", [128, 128])
        w_qkv = {s: sb(f"w_qkv_{s}", [CH, 3 * CH]) for s in "AB"}
        w_proj = {s: sb(f"w_proj_{s}", [CH, CH]) for s in "AB"}
        b_qkv = {s: sb(f"b_qkv_{s}", [CH, 3]) for s in "AB"}
        b_proj = {s: sb(f"b_proj_{s}", [CH, 1]) for s in "AB"}
        b_q_scaled = {s: sb(f"b_q_scaled_{s}", [CH, 1]) for s in "AB"}
        mask_tab = sb("mask_tab", [128, 2 * PAIRS * N])
        bias_tab = sb("bias_tab", [128, HEADS * N])
        minus_half = sb("minus_half", [128, 1])
        eps = sb("eps", [128, 1])
        idle_dve = sb("idle_dve", [128, 1])
        zero = sb("zero", [128, 1])

        xr = sb("xr", [128, RING * IMG])
        x1r = sb("x1r", [128, RING * IMG])
        x_in = [sb(f"x_in{i}", [PT, JT * CH]) for i in range(2)]
        xn = [sb(f"xn{i}", [128, WINS * WPAD]) for i in range(2)]
        q_t = sb("q_t", [128, TOK])
        k_t = sb("k_t", [128, TOK])
        v_bd = [sb(f"v_bd{i}", [128, 2, 2, HEADS, 2, VW]) for i in range(2)]
        logits = sb("logits", [128, HEADS, PAIRS, N])
        neg_max = sb("neg_max", [128, HEADS, PAIRS])
        probs = sb("probs", [128, HEADS, PAIRS, WPAD])
        probs_t = sb("probs_t", [128, 2, 2, 2, 2, N])
        sums = sb("sums", [128, 2, HEADS * 2])
        inv_sums = sb("inv_sums", [128, 2, HEADS * 2])
        o_sb = sb("o_sb", [128, PAIRS, CH])
        o_t = sb("o_t", [128, TOK])
        y_t = sb("y_t", [128, TOK])
        out_st = sb("out_st", [PT, JT * CH])
        bn = {s: sb(f"bn_{s}", [128, STRIPS * 6]) for s in "AB"}
        chan = {s: sb(f"chan_{s}", [128, 2]) for s in "AB"}
        gmean = {s: sb(f"gmean_{s}", [128, 1]) for s in "AB"}
        dev = {s: sb(f"dev_{s}", [128, 1]) for s in "AB"}
        dev2 = {s: sb(f"dev2_{s}", [128, 1]) for s in "AB"}
        spread = {s: sb(f"spread_{s}", [128, 1]) for s in "AB"}
        gvar = {s: sb(f"gvar_{s}", [128, 1]) for s in "AB"}
        grstd = {s: sb(f"grstd_{s}", [128, 1]) for s in "AB"}
        cur_mean = {s: sb(f"cur_mean_{s}", [128, 1]) for s in "AB"}
        cur_rstd = {s: sb(f"cur_rstd_{s}", [128, 1]) for s in "AB"}

        consts_in = sem("consts_in")
        bias_in = sem("bias_in")
        buffers_set = sem("buffers_set")
        banks_set = sem("banks_set")
        x_loaded = [sem(f"x_loaded{i}") for i in range(2)]
        x_swapped = sem("x_swapped")
        x_stored = sem("x_stored")
        x_padded = sem("x_padded")
        x1_padded = sem("x1_padded")
        norm_done = sem("norm_done")
        q_done, k_done, v_done = sem("q_done"), sem("k_done"), sem("v_done")
        q_copied, k_copied = sem("q_copied"), sem("k_copied")
        v_copied0, v_copied1 = sem("v_copied0"), sem("v_copied1")
        scores_done = sem("scores_done")
        biased = sem("biased")
        max_done = sem("max_done")
        shifted = sem("shifted")
        exp_done = sem("exp_done")
        pt_done, pt_copied = sem("pt_done"), sem("pt_copied")
        o_done = sem("o_done")
        sums_safe, sums_inverted = sem("sums_safe"), sem("sums_inverted")
        o_scaled = sem("o_scaled")
        ot_done, ot_copied = sem("ot_done"), sem("ot_copied")
        y_done, y_taken = sem("y_done"), sem("y_taken")
        x1_written = sem("x1_written")
        y_swapped, y_staged, y_stored = sem("y_swapped"), sem("y_staged"), sem("y_stored")
        bn_done = {s: sem(f"bn_done_{s}") for s in "AB"}
        chan_done = {s: sem(f"chan_done_{s}") for s in "AB"}
        gmean_mm = {s: sem(f"gmean_mm_{s}") for s in "AB"}
        gmean_out = {s: sem(f"gmean_out_{s}") for s in "AB"}
        spread_out = {s: sem(f"spread_out_{s}") for s in "AB"}
        gvar_mm = {s: sem(f"gvar_mm_{s}") for s in "AB"}
        gvar_out = {s: sem(f"gvar_out_{s}") for s in "AB"}
        pool_step = sem("pool_step")
        stats_cur = {s: sem(f"stats_cur_{s}") for s in "AB"}

        def stat_matmul(pe, s, image):
            at_least(pe, chan_done[s], image + 1)
            nc.tensor.matmul(stat_col, group_avg[:, :], chan[s][:, 0:1], start=True, stop=True)\
                .then_inc(gmean_mm[s], 1)

        def spread_matmul(pe, s, image):
            at_least(pe, spread_out[s], image + 1)
            nc.tensor.matmul(stat_col, group_avg[:, :], spread[s][:, :], start=True, stop=True)\
                .then_inc(gvar_mm[s], 1)

        def mean_copy(act, s, image):
            at_least(act, gmean_mm[s], image + 1)
            nc.scalar.copy(gmean[s][:, :], stat_col).then_inc(gmean_out[s], 1)

        def var_copy(act, s, image):
            at_least(act, gvar_mm[s], image + 1)
            nc.scalar.activation(gvar[s][:, :], stat_col, ACT.Identity, bias=eps[:, :]).then_inc(gvar_out[s], 1)

        def image_before(t):
            return (t >> 3) - 1

        def v_half(step, a):
            src = v_bank[a * WPAD:(a + 1) * WPAD, :].rearrange("p (g h d) -> p g h d", g=4, h=HEADS)
            dst = v_bd[step.parity][a * WPAD:(a + 1) * WPAD].rearrange("p b w h a v -> p (b w) h a v")
            return dst[:, :, :, a, 0:HD], src

        def slot_of(c, parity=0):
            return c % 2 if isinstance(c, int) else parity

        block = ctx.enter_context(nc.Block())

        @block.sync
        def _(sp):
            def chunk(images, k):
                at = k * (TOK * CH)
                return bass.AP(images.tensor, at if isinstance(k, int) else sp.snap(at),
                               [[JT * CH, PT], [1, JT * CH]])

            def load(c, k, slot, swapped):
                src = chunk(x, k)
                if not isinstance(swapped, int):
                    swapped = sp.snap(swapped)
                at_least(sp, x_swapped, swapped)
                sp.dma_start(x_in[slot][:, :], src).then_inc(x_loaded[slot], 16)

            for slot in range(2):
                load(slot, slot, slot, 0)
            sp.dma_start(ident[:, :], ident_in).then_inc(consts_in, 16)
            sp.dma_start(group_avg[:, :], group_in).then_inc(consts_in, 16)
            for s in "AB":
                sp.dma_start(w_qkv[s][:, :], qkv_w[s]).then_inc(consts_in, 16)
                sp.dma_start(w_proj[s][:, :], proj_w[s]).then_inc(consts_in, 16)
                sp.dma_start(b_qkv[s][:, :], qkv_b[s].rearrange("(t p) -> p t", p=CH)).then_inc(consts_in, 16)
                sp.dma_start(b_proj[s][:, :], proj_b[s].rearrange("(p o) -> p o", o=1)).then_inc(consts_in, 16)
            sp.dma_start(mask_tab[:, :], mask).then_inc(consts_in, 16)
            def relative_bias(q):
                first = (WS - 1 - q // WS) * TABLE_SIDE + WS - 1 - q % WS
                src = bass.AP(bias_rev.tensor, bias_rev.offset + first,
                              [[TABLE_SIDE ** 2, 1], [TABLE_SIDE ** 2, HEADS], [TABLE_SIDE, WS], [1, WS]])
                dst = bias_tab[q:q + 1, :].rearrange("p (h a b) -> p h a b", h=HEADS, a=WS)
                sp.dma_start(dst, src).then_inc(bias_in, 16)

            for c in range(2, LEAD + 1):
                load(c, c, c % 2, c - 1)
                if c == 2:
                    sp.wait_ge(buffers_set, 1)
                for q in range((c - 2) * 4, min((c - 1) * 4, N)):
                    relative_bias(q)
            sp.wait_ge(bias_in, N * 16)
            sp.dma_start(bias_tab[WPAD:WPAD + N, :], bias_tab[0:N, :]).then_inc(bias_in, 16)

            def step(before, prev, cur, nxt, after):
                if cur is not None and cur.stream == "A":
                    c = cur.strip + LEAD + 1
                    if isinstance(c, int):
                        if c < TOTAL + LEAD:
                            paired = c < LAG + LEAD
                            load(c, c % TOTAL, c % 2 if paired else 0, c - 1 if paired else c)
                    elif cur.part == 0:
                        load(c, c, 1 - cur.parity, c - 1)
                    else:
                        load(c, c % TOTAL, 0, c)
                if before is not None and before.stream == "B":
                    m = before.strip
                    at_least(sp, y_staged, m + 1)
                    sp.dma_start(chunk(out, m), out_st[:, :]).then_inc(y_stored, 16)
            walk(sp, step)
            sp.wait_ge(y_stored, TOTAL * 16)

        @block.gpsimd
        def _(pool):
            nc.gpsimd.memset(zero[:, :], 0.0)
            nc.gpsimd.memset(minus_half[:, :], -0.5).then_inc(pool_step, 1)
            pool.wait_ge(pool_step, 1)

            def pad_image(ring, img, done, to_low):
                off = img % RING * IMG
                own = SHIFT if to_low else 0
                for r0, c0, n, width, dr, dc in ((own, 0, SIDE, SHIFT, 0, 1), (0, own, SHIFT, SIDE, 1, 0),
                                                 (0, 0, SHIFT, SHIFT, 1, 1)):
                    first = rows(ring, off + r0 * PITCH, c0, width, n)
                    second = rows(ring, off + (r0 + dr * SIDE) * PITCH, c0 + dc * SIDE, width, n)
                    dst, src = (first, second) if to_low else (second, first)
                    nc.gpsimd.tensor_copy(dst, src).then_inc(done, 1)

            def finish_stats(s, img, before):
                pool.wait_ge(gmean_out[s], img + 1)
                nc.gpsimd.tensor_tensor(dev[s][:, :], chan[s][:, 0:1], gmean[s][:, :], ALU.subtract)\
                    .then_inc(pool_step, 1)
                pool.wait_ge(pool_step, before + 1)
                nc.gpsimd.tensor_tensor(dev2[s][:, :], dev[s][:, :], dev[s][:, :], ALU.mult)\
                    .then_inc(pool_step, 1)
                pool.wait_ge(pool_step, before + 2)
                nc.gpsimd.tensor_tensor(spread[s][:, :], dev2[s][:, :], chan[s][:, 1:2], ALU.add)\
                    .then_inc(spread_out[s], 1)
                pool.wait_ge(gvar_out[s], img + 1)
                nc.gpsimd.tensor_tensor(grstd[s][:, :], gvar[s][:, :], minus_half[:, :], ALU.pow)\
                    .then_inc(pool_step, 1)
                pool.wait_ge(pool_step, before + 3)

            def publish(s, normed):
                for to, of in ((cur_mean[s], gmean[s]), (cur_rstd[s], grstd[s])):
                    at_least(pool, norm_done, normed)
                    nc.gpsimd.tensor_tensor(to[:, :], of[:, :], zero[:, :], ALU.add).then_inc(stats_cur[s], 1)

            pool.wait_ge(x_stored, STRIPS)
            pad_image(xr, 0, x_padded, False)
            finish_stats("A", 0, 1)
            publish("A", 0)
            pool.wait_ge(x_stored, 2 * STRIPS)
            pad_image(xr, 1, x_padded, False)

            def image(i, before, a_normed, b_normed):
                finish_stats("A", i + 1, before)
                if b_normed is not None:
                    pool.wait_ge(x1_written, i * STRIPS)
                    pad_image(x1r, i - 1, x1_padded, True)
                    finish_stats("B", i - 1, before + 3)
                publish("A", a_normed)
                if b_normed is not None:
                    publish("B", b_normed)
                pool.wait_ge(x_stored, (i + 3) * STRIPS)
                pad_image(xr, i + 2, x_padded, False)

            image(0, 4, STRIPS, None)
            image(1, 7, 2 * STRIPS, 0)
            with pool.Fori(2, IMAGES) as i:
                image(i, i * 6 + 1, i * 16 - 1, i * 16)
            pool.wait_ge(x1_written, TOTAL)
            pad_image(x1r, IMAGES - 1, x1_padded, True)
            finish_stats("B", IMAGES - 1, IMAGES * 6 + 1)
            publish("B", STEPS - STRIPS)

        @block.scalar
        def _(act):
            act.wait_ge(consts_in, 16 * 11)
            act.wait_ge(buffers_set, 2)
            act.wait_ge(banks_set, 1)

            def store_chunk(c, with_stats, step=None):

                def after_swap(copy, s, image):
                    at_least(act, x_swapped, c + 1)
                    copy(act, s, image)
                if step is not None:
                    at_time(act, step, X1_MEAN, lambda: after_swap(mean_copy, "B", image_before(step.g)))
                    at_time(act, step, X1_VAR, lambda: after_swap(var_copy, "B", image_before(step.g)))
                if with_stats:
                    when(act, c & 7, X_MEAN, lambda: after_swap(mean_copy, "A", image_before(c)))
                    when(act, c & 7, X_VAR, lambda: after_swap(var_copy, "A", image_before(c)))
                dst = rows(xr, ring_at(act, c), 0)
                dst = bass.AP(dst.tensor, dst.offset, [dst.ap[0], [PITCH, WS], [JT, SIDE // JT], [1, JT]])
                src = swap_bank[:, 0:TOK].rearrange("p (j r q) -> p r q j", j=JT, r=WS)
                at_least(act, x_swapped, c + 1)
                nc.scalar.copy(dst, src).then_inc(x_stored, 1)

            with act.Fori(0, STRIPS) as c:
                store_chunk(c, False)
            with act.Fori(STRIPS, LEAD) as c:
                store_chunk(c, True)

            def step(before, prev, cur, nxt, after):
                if nxt is not None:
                    s = nxt.stream
                    at_least(act, q_done, nxt.n + 1)
                    nc.scalar.activation(q_t[:, :], q_bank[:, 0:TOK], ACT.Identity,
                                         bias=b_q_scaled[s][:, :], scale=SCALE[s]).then_inc(q_copied, 1)
                    at_least(act, k_done, nxt.n + 1)
                    nc.scalar.activation(k_t[:, :], k_bank[:, 0:TOK], ACT.Identity,
                                         bias=b_qkv[s][:, 1:2]).then_inc(k_copied, 1)
                if cur is not None:
                    for hp in range(2):
                        at_least(act, pt_done, cur.n * 2 + hp + 1)
                        src = score_banks[:, hp, :].rearrange("p (b q) -> p b q", q=WPAD)[:, :, 0:N]
                        dst = probs_t[:, hp].rearrange("p a b w q -> p (a b w) q")
                        nc.scalar.copy(dst, src).then_inc(pt_copied, 1)
                if cur is not None and cur.stream == "A":
                    store_chunk(cur.strip + LEAD, True, cur)
                else:
                    at_time(act, cur, X1_MEAN, lambda: mean_copy(act, "B", image_before(cur.g)))
                    at_time(act, cur, X1_VAR, lambda: var_copy(act, "B", image_before(cur.g)))
                if before is not None and before.stream == "B":
                    m = before.strip
                    at_least(act, y_stored, m * 16)
                    at_least(act, y_swapped, m + 1)
                    nc.scalar.copy(out_st[:, :], score_banks[0:PT, 2, :]).then_inc(y_staged, 1)
                if nxt is not None:
                    at_least(act, v_done, nxt.n + 1)
                    nc.scalar.copy(*v_half(nxt, 0)).then_inc(v_copied0, 1)
                if prev is not None:
                    at_least(act, ot_done, prev.n + 1)
                    src = ot_bank[:, :].rearrange("p (w q) -> p w q", q=WPAD)[:, :, 0:N]\
                        .rearrange("p w (i j) -> p w i j", j=WS)
                    dst = o_t[:, :].rearrange("p (i w j) -> p w i j", w=WINS, j=WS)
                    nc.scalar.activation(dst, src, ACT.Identity, bias=b_qkv[prev.stream][:, 2:3])\
                        .then_inc(ot_copied, 1)
                if nxt is not None:
                    for hp in range(2):
                        at_least(act, shifted, nxt.n * 2 + hp + 1)
                        heads = slice(2 * hp, 2 * hp + 2)
                        nc.scalar.activation(
                            probs[:, heads].rearrange("p h j k -> p (h j) k")[:, :, 0:N],
                            logits[:, heads].rearrange("p h j k -> p (h j) k"), ACT.Exp).then_inc(exp_done, 1)
            walk(act, step)

        @block.vector
        def _(dve):
            for buf in (bias_tab, probs, xn[0], xn[1], v_bd[0]):
                shape = " ".join("abcdefg"[:len(buf.shape) - 1])
                nc.vector.memset(buf[:].rearrange(f"p {shape} -> p ({shape})"), 0.0)
            nc.vector.memset(v_bd[1][:].rearrange("p a b c d e -> p (a b c d e)"), 0.0).then_inc(buffers_set, 1)
            dve.wait_ge(buffers_set, 1)
            nc.vector.memset(eps[:, :], GN_EPS)
            for i in range(2):
                for a in range(2):
                    ones = v_bd[i][a * WPAD:(a + 1) * WPAD].rearrange("p b w h a v -> p (b w h) a v")
                    nc.vector.memset(ones[:, :, a, HD:VW], 1.0)
            dve.wait_ge(consts_in, 16 * 11)
            nc.vector.tensor_scalar(b_q_scaled["A"][:, :], b_qkv["A"][:, 0:1], SCALE["A"], None, ALU.mult)
            nc.vector.tensor_scalar(b_q_scaled["B"][:, :], b_qkv["B"][:, 0:1], SCALE["B"], None, ALU.mult)\
                .then_inc(buffers_set, 1)
            for b in (q_bank, k_bank, v_bank, ot_bank):
                nc.vector.memset(b[:, :], 0.0)
            nc.vector.memset(score_banks[:, :, :].rearrange("p h c -> p (h c)"), 0.0).then_inc(banks_set, 1)

            def chunk_stats(c):
                at_least(dve, x_stored, c + 1)
                nc.vector.bn_stats(bn["A"][:, bass.ds((c & 7) * 6, 6)], rows(xr, ring_at(dve, c), 0))\
                    .then_inc(bn_done["A"], 1)

            def channel_stats(s, count):
                at_least(dve, bn_done[s], count)
                nc.vector.memset(idle_dve[:, :], 0.0)
                nc.vector.bn_aggr(chan[s][:, :], bn[s][:, :]).then_inc(chan_done[s], 1)

            for first in (0, STRIPS):
                with dve.Fori(first, first + STRIPS) as c:
                    chunk_stats(c)
                if first == 0:
                    channel_stats("A", STRIPS)
            dve.wait_ge(stats_cur["A"], 2)
            channel_stats("A", 2 * STRIPS)

            def normalise(st):
                s, strip = st.stream, st.strip
                at_least(dve, v_done, st.n - 1)
                img = strip >> 3
                at_least(dve, stats_cur[s], img * 2 + 2)
                at_least(dve, x_padded if s == "A" else x1_padded, img * 3 + 3)
                off = ring_at(dve, strip)
                start = SHIFT * PITCH + SHIFT if s == "A" else 0
                v = rows(xr if s == "A" else x1r, off + start, 0)
                src = bass.AP(v.tensor, v.offset, [v.ap[0], [WS, WINS], [PITCH, WS], [1, WS]])
                dst = xn[st.parity][:, :].rearrange("p (w q) -> p w q", q=WPAD)[:, :, 0:N]\
                    .rearrange("p w (i j) -> p w i j", j=WS)
                nc.vector.tensor_scalar(dst, src, cur_mean[s][:, :], cur_rstd[s][:, :],
                                        ALU.subtract, ALU.mult).then_inc(norm_done, 1)

            def scores_to_logits(st):
                for hp in range(2):
                    heads = slice(2 * hp, 2 * hp + 2)
                    n = st.n * 2 + hp + 1
                    if st.stream == "A":
                        last = (st.strip & 7) + 1 >> 3
                        
                        table = mask_tab[:, bass.ds(last * (PAIRS * N), PAIRS * N)]
                        table = bass.AP(table.tensor, table.offset, [table.ap[0], [0, 2], [1, PAIRS * N]])
                        src = score_banks[:, heads, 0:PAIRS * N]
                        dst = logits[:, heads].rearrange("p h j k -> p h (j k)")
                    else:
                        if hp == 0:
                            at_least(dve, bias_in, (N + 1) * 16)
                        table = bias_tab[:, 2 * hp * N:(2 * hp + 2) * N]
                        table = bass.AP(table.tensor, table.offset, [table.ap[0], [N, 2], [0, PAIRS], [1, N]])
                        src = score_banks[:, heads, 0:PAIRS * N].rearrange("p h (j k) -> p h j k", k=N)
                        dst = logits[:, heads]
                    at_least(dve, scores_done, n)
                    nc.vector.tensor_tensor(dst, src, table, ALU.add).then_inc(biased, 1)
                    at_least(dve, biased, n)
                    rows_of = logits[:, heads].rearrange("p h j k -> p (h j) k")
                    top = neg_max[:, heads].rearrange("p h j -> p (h j)")
                    nc.vector.tensor_reduce(top, rows_of, AX.X, ALU.max, negate=True).then_inc(max_done, 1)
                    at_least(dve, max_done, n)
                    nc.vector.tensor_tensor(
                        rows_of, rows_of,
                        bass.AP(top.tensor, top.offset, [top.ap[0], [1, 2 * PAIRS], [0, N]]),
                        ALU.add).then_inc(shifted, 1)

            def add_residual(st):
                s = st.stream
                off = ring_at(dve, st.strip)
                at_least(dve, y_done, st.n + 1)
                y = y_bank[:, 0:TOK].rearrange("p (i c) -> p i c", i=WS)
                if s == "A":
                    place = off + SHIFT * PITCH
                    nc.vector.scalar_tensor_tensor(
                        rows(x1r, place, SHIFT), y, b_proj[s][:, :], rows(xr, place, SHIFT),
                        ALU.add, ALU.add).then_inc(y_taken, 1)
                    at_least(dve, y_taken, st.n + 1)
                    nc.vector.bn_stats(bn[s_x1][:, bass.ds((st.strip & 7) * 6, 6)],
                                       rows(x1r, place, SHIFT)).then_inc(x1_written, 1)
                else:
                    nc.vector.scalar_tensor_tensor(
                        y_t[:, :].rearrange("p (i c) -> p i c", i=WS), y, b_proj[s][:, :],
                        rows(x1r, off, 0), ALU.add, ALU.add).then_inc(y_taken, 1)
            s_x1 = "B"

            def scale_outputs(st):
                for pp in range(2):
                    n = st.n * 2 + pp + 1
                    o = o_banks[pp][:, 0:HEADS * 2 * VW].rearrange("p (g v) -> p g v", v=VW)
                    at_least(dve, o_done, n)
                    nc.vector.tensor_scalar(sums[:, pp, :], o[:, :, HD], 0.5, None, ALU.max)\
                        .then_inc(sums_safe, 1)
                    at_least(dve, sums_safe, n)
                    nc.vector.reciprocal(inv_sums[:, pp, :], sums[:, pp, :]).then_inc(sums_inverted, 1)
                    at_least(dve, sums_inverted, n)
                    inv = inv_sums[:, pp, :]
                    inv = bass.AP(inv.tensor, inv.offset, [inv.ap[0], [2, HEADS], [1, 2], [0, HD]])
                    nc.vector.tensor_tensor(
                        o_sb[:, 2 * pp:2 * pp + 2, :].rearrange("p a (h d) -> p h a d", h=HEADS),
                        o[:, :, 0:HD].rearrange("p (h a) d -> p h a d", h=HEADS), inv, ALU.mult)\
                        .then_inc(o_scaled, 1)

            def step(before, prev, cur, nxt, after):
                if nxt is not None:
                    at_least(dve, v_done, nxt.n + 1)
                    nc.vector.tensor_copy(*v_half(nxt, 1)).then_inc(v_copied1, 1)
                chunk = cur.strip + LEAD if cur is not None and cur.stream == "A" else None
                if chunk is not None:
                    chunk_stats(chunk)
                if after is not None:
                    normalise(after)
                if chunk is not None:
                    when(dve, chunk & 7, STRIPS - 1, lambda: channel_stats("A", chunk + 1))
                if nxt is not None:
                    scores_to_logits(nxt)
                if prev is not None:
                    add_residual(prev)
                at_time(dve, cur, X1_CHAN, lambda: channel_stats_x1(cur))
                if cur is not None:
                    scale_outputs(cur)

            def channel_stats_x1(cur):
                at_least(dve, x1_written, (cur.g >> 3) * STRIPS)
                nc.vector.memset(idle_dve[:, :], 0.0)
                nc.vector.bn_aggr(chan["B"][:, :], bn["B"][:, :]).then_inc(chan_done["B"], 1)
            walk(dve, step)

        @block.tensor
        def _(pe):
            pe.wait_ge(consts_in, 16 * 11)
            pe.wait_ge(banks_set, 1)
            pe.wait_ge(buffers_set, 2)

            def swap_chunk(c, slot, loaded, with_stats):
                if with_stats:
                    when(pe, c & 7, X_MEAN, lambda: stat_matmul(pe, "A", image_before(c)))
                    when(pe, c & 7, X_VAR, lambda: spread_matmul(pe, "A", image_before(c)))
                at_least(pe, x_loaded[slot], loaded)
                for j in range(JT):
                    last = nc.tensor.transpose(swap_bank[:, j * PT:(j + 1) * PT],
                                               x_in[slot][:, j * CH:(j + 1) * CH], ident[0:PT, 0:PT])
                last.then_inc(x_swapped, 1)

            def first_chunks(half_c):
                for slot in range(2):
                    c = half_c * 2 + slot
                    at_least(pe, x_stored, c)
                    swap_chunk(c, slot, half_c * 16 + 16, not isinstance(c, int))

            first_chunks(0)
            with pe.Fori(1, LEAD // 2) as half_c:
                first_chunks(half_c)
            pe.wait_ge(x_stored, LEAD)

            def step(before, prev, cur, nxt, after):
                if nxt is not None:
                    w, tokens = w_qkv[nxt.stream], xn[nxt.parity]
                    moving = tokens[:, :].rearrange("p (w q) -> p w q", q=WPAD)[:, :, 0:N]
                    at_least(pe, norm_done, nxt.n + 1)
                    at_least(pe, q_copied, nxt.n)
                    nc.tensor.matmul(q_bank[:, 0:TOK], w[:, 0:CH], moving, start=True, stop=True)\
                        .then_inc(q_done, 1)
                    at_least(pe, y_taken, nxt.n - 2)
                    nc.tensor.matmul(k_bank[:, 0:TOK], w[:, CH:2 * CH], moving, start=True, stop=True)\
                        .then_inc(k_done, 1)
                if cur is not None:
                    for hp in range(2):
                        at_least(pe, exp_done, cur.n * 2 + hp + 1)
                        for h2 in range(2):
                            for pp in range(2):
                                b = h2 * 2 + pp
                                last = nc.tensor.transpose(
                                    score_banks[:, hp, b * 128:(b + 1) * 128],
                                    probs[:, 2 * hp + h2, 2 * pp:2 * pp + 2, :].rearrange("p j k -> p (j k)"),
                                    ident[:, :])
                        last.then_inc(pt_done, 1)
                if cur is not None:
                    image = image_before(cur.g)

                    def mean_b():
                        stat_matmul(pe, "B", image)
                        if cur.stream == "B":
                            at_least(pe, gmean_out["B"], image + 1)

                    def var_b():
                        spread_matmul(pe, "B", image)
                        if cur.stream == "B":
                            at_least(pe, gvar_out["B"], image + 1)
                    at_time(pe, cur, X1_MEAN, mean_b)
                    at_time(pe, cur, X1_VAR, var_b)
                if cur is not None and cur.stream == "A":
                    c = cur.strip + LEAD
                    if cur.part == 0:
                        slot = cur.parity
                        loaded = ((c >> 1) + 1) * 16
                    else:
                        slot = 0
                        loaded = (c - (LAG + LEAD) // 2 + 1) * 16
                    swap_chunk(c, slot, loaded, True)
                if before is not None and before.stream == "B":
                    at_least(pe, y_taken, before.n + 1)
                    for j in range(JT):
                        last = nc.tensor.transpose(score_banks[0:PT, 2, j * CH:(j + 1) * CH],
                                                   y_t[:, j::JT], ident[:, :])
                    last.then_inc(y_swapped, 1)
                if nxt is not None:
                    at_least(pe, o_scaled, (nxt.n - 2) * 2 + 1)
                    for b in range(WINS // 2):
                        last = nc.tensor.matmul(v_bank[:, b * CH:(b + 1) * CH],
                                                tokens[:, b * 2 * WPAD:(b + 1) * 2 * WPAD],
                                                w[:, 2 * CH:3 * CH], start=True, stop=True)
                    last.then_inc(v_done, 1)
                if prev is not None:
                    at_least(pe, o_scaled, prev.n * 2 + 2)
                    for j in range(PAIRS):
                        first = (4 * (j // 2) + j % 2) * WPAD
                        dst = ot_bank[:, first:first + 3 * WPAD]
                        dst = bass.AP(dst.tensor, dst.offset, [dst.ap[0], [2 * WPAD, 2], [1, WPAD]])
                        last = nc.tensor.transpose(dst, o_sb[:, j, :], ident[:, :])
                    last.then_inc(ot_done, 1)
                if nxt is not None:
                    at_least(pe, q_copied, nxt.n + 1)
                    at_least(pe, k_copied, nxt.n + 1)
                    at_least(pe, pt_copied, nxt.n * 2)
                    for hp in range(2):
                        if hp == 1:
                            if cur is not None and cur.stream == "A":
                                at_least(pe, x_stored, cur.strip + LEAD + 1)
                            if before is not None and before.stream == "B":
                                at_least(pe, y_staged, before.strip + 1)
                        for win in range(WINS):
                            j, half = place(win)
                            for h in (2 * hp, 2 * hp + 1):
                                last = nc.tensor.matmul(
                                    score_banks[half * WPAD:half * WPAD + N, h, j * N:(j + 1) * N],
                                    q_t[h * HD:(h + 1) * HD, win * N:(win + 1) * N],
                                    k_t[h * HD:(h + 1) * HD, win * N:(win + 1) * N], start=True, stop=True)
                        last.then_inc(scores_done, 1)
                if prev is not None:
                    at_least(pe, ot_copied, prev.n + 1)
                    nc.tensor.matmul(y_bank[:, 0:TOK], w_proj[prev.stream][:, :], o_t[:, :],
                                     start=True, stop=True).then_inc(y_done, 1)
                if cur is not None:
                    at_least(pe, pt_copied, cur.n * 2 + 2)
                    if nxt is not None:
                        at_least(pe, v_copied0, nxt.n + 1)
                        at_least(pe, v_copied1, nxt.n + 1)
                    for pp in range(2):
                        for h in range(HEADS):
                            for half in range(2):
                                last = nc.tensor.matmul(
                                    o_banks[pp][half * WPAD:half * WPAD + N, h * 2 * VW:(h + 1) * 2 * VW],
                                    probs_t[:, h // 2, h % 2, pp, half, :],
                                    v_bd[cur.parity][:, pp, half, h].rearrange("p a v -> p (a v)"),
                                    start=True, stop=True)
                        last.then_inc(o_done, 1)
            walk(pe, step)


def kernel(x, L0_conv_qkv_w, L0_conv_qkv_b, L0_conv_proj_w, L0_conv_proj_b,
           L1_conv_qkv_w, L1_conv_qkv_b, L1_conv_proj_w, L1_conv_proj_b, L1_conv_bias_table):
    import numpy as np
    import concourse.bacc as bacc
    from concourse.bass_utils import run_bass_kernel_spmd

    region = np.zeros((SIDE, SIDE), np.int32)
    cuts = (slice(0, -WS), slice(-WS, -SHIFT), slice(-SHIFT, None))
    for a, rs in enumerate(cuts):
        for b, cs in enumerate(cuts):
            region[rs, cs] = 3 * a + b
    mask = np.zeros((128, 2, PAIRS, N), np.float32)
    for last in range(2):
        for win in range(WINS):
            r = region[(STRIPS - 1) * last * WS:((STRIPS - 1) * last + 1) * WS,
                       win * WS:(win + 1) * WS].reshape(-1)
            pair, half = place(win)
            q = half * WPAD
            mask[q:q + N, last, pair] = np.where(r[:, None] != r[None, :], -1e9, 0.0)

    feeds = {
        "x": x, "mask": mask.reshape(128, -1), "ident": np.eye(128, dtype=np.float32),
        "group": np.kron(np.eye(GROUPS), np.full((CH // GROUPS,) * 2, GROUPS / CH)).astype(np.float32),
        "bias_rev": np.ascontiguousarray(np.asarray(L1_conv_bias_table)[::-1].T),
        "qkv_w_A": L0_conv_qkv_w, "qkv_b_A": L0_conv_qkv_b, "proj_w_A": L0_conv_proj_w, "proj_b_A": L0_conv_proj_b,
        "qkv_w_B": L1_conv_qkv_w, "qkv_b_B": L1_conv_qkv_b, "proj_w_B": L1_conv_proj_w, "proj_b_B": L1_conv_proj_b,
    }
    feeds = {k: np.ascontiguousarray(v) for k, v in feeds.items()}
    nc = bacc.Bacc("TRN2", target_bir_lowering=False, num_devices=1)
    d = {k: nc.dram_tensor(f"in_{k}", v.shape, mybir.dt.from_np(v.dtype), kind="ExternalInput").ap()
         for k, v in feeds.items()}
    out = nc.dram_tensor("out", feeds["x"].shape, F32, kind="ExternalOutput").ap()
    window_attention_layers(
        nc, d["x"], {s: d[f"qkv_w_{s}"] for s in "AB"}, {s: d[f"qkv_b_{s}"] for s in "AB"},
        {s: d[f"proj_w_{s}"] for s in "AB"}, {s: d[f"proj_b_{s}"] for s in "AB"},
        d["bias_rev"], d["mask"], d["ident"], d["group"], out)
    r = run_bass_kernel_spmd(nc, [{f"in_{k}": v for k, v in feeds.items()}], core_ids=[0])
    return r.results[0]["out"]
```

```python
from contextlib import ExitStack

import concourse.bass as bass
from concourse import mybir

F32 = mybir.dt.float32
ACT = mybir.ActivationFunctionType
ALU = mybir.AluOpType
AX = mybir.AxisListType

IMAGES, SIDE, CH = 64, 56, 128
WS, SHIFT, HEADS, GROUPS = 7, 3, 4, 32
HD = CH // HEADS
N = WS * WS
WPAD = 64
WINS = SIDE // WS
PAIRS = WINS // 2
STRIPS = SIDE // WS
TOK = WINS * N
PITCH = SIDE + SHIFT
ROWS_STRIP = WS * PITCH
IMG = PITCH * PITCH
RING = 3
TOTAL = IMAGES * STRIPS
LAG = 2 * STRIPS
LEAD = 2 * STRIPS
JT = 4
PT = TOK // JT
VW = HD + 1
GN_EPS = 1e-5
TABLE_SIDE = 2 * WS - 1
SCALE = {"A": float(CH) ** -0.5, "B": float(HD) ** -0.5}

STEPS = 2 * TOTAL
ALONE = LAG
HP_ORDER = (1, 0)
SCHEDULE = [(-2, 2, False), (2, ALONE - 2, True), (ALONE - 2, ALONE + 4, False),
            (ALONE + 4, STEPS - ALONE - 2, True), (STEPS - ALONE - 2, STEPS - ALONE + 2, False),
            (STEPS - ALONE + 2, STEPS - 2, True), (STEPS - 2, STEPS + 2, False)]


def place(win):
    pp, w, a = win // 4, win // 2 % 2, win % 2
    return 2 * pp + a, w


class Step:

    def __init__(self, n, stream, strip, parity, part):
        self.n, self.stream, self.strip = n, stream, strip
        self.parity = parity
        self.part = part
        self.g = strip if stream == "A" else strip + LAG
        self.leads = stream == "A" or part == 2


def step_at(u):
    if u < 0 or u >= STEPS:
        return None
    if u < ALONE:
        return Step(u, "A", u, u % 2, 0)
    if u >= STEPS - ALONE:
        return Step(u, "B", u - TOTAL, u % 2, 2)
    if u % 2 == 0:
        return Step(u, "A", LAG + (u - ALONE) // 2, 0, 1)
    return Step(u, "B", (u - ALONE) // 2, 1, 1)


def later(step, it):
    rate = 1 if step.part == 1 else 2
    return Step(step.n + it * 2, step.stream, step.strip + it * rate, step.parity, step.part)


def walk(eng, body):
    for lo, hi, looped in SCHEDULE:
        if looped:
            with eng.Fori(0, (hi - lo) // 2) as it:
                for u in (lo, lo + 1):
                    body(*[later(step_at(u + k), it) for k in (-2, -1, 0, 1, 2)])
        else:
            for u in range(lo, hi):
                body(*[step_at(u + k) for k in (-2, -1, 0, 1, 2)])


def at_least(eng, sem, value):
    if not isinstance(value, int) or value > 0:
        eng.wait_ge(sem, value)


def when(eng, value, wanted, body):
    if isinstance(value, int):
        if value == wanted:
            body()
    else:
        with eng.If(value == wanted):
            body()


def ring_at(eng, strip):
    r = strip % (RING * STRIPS)
    gap = IMG - STRIPS * ROWS_STRIP
    if isinstance(strip, int):
        return r * ROWS_STRIP + (r // STRIPS) * gap
    r = eng.snap(r)
    return eng.snap(r * ROWS_STRIP + (r >> 3) * gap).with_bounds(min_val=0, max_val=RING * IMG - gap - ROWS_STRIP)


def rows(ring, off, col, width=SIDE, n=WS):
    v = ring[:, bass.ds(off + col, (n - 1) * PITCH + width)]
    return bass.AP(v.tensor, v.offset, [v.ap[0], [PITCH, n], [1, width]])


CHAN, MEAN, VAR = 0, 1, 5


def at_phase(eng, step, phases, body, first_x=0, order="AB"):
    if step is None or not step.leads:
        return
    g = step.g
    x_image, x1_image = (g >> 3) + 1, (g >> 3) - 1

    def both(phase):
        for s in order:
            body(phase, s, x_image if s == "A" else x1_image)
    if isinstance(g, int):
        if g % STRIPS in phases:
            for s in order:
                if s == "A" and first_x <= g < TOTAL:
                    body(g % STRIPS, "A", x_image)
                if s == "B" and STRIPS <= g < TOTAL + STRIPS:
                    body(g % STRIPS, "B", x1_image)
    elif step.part == 1 and len(phases) == 1:
        when(eng, g & (STRIPS - 1), phases[0], lambda: both(phases[0]))
    elif step.part == 1:
        when(eng, g & 3, MEAN & 3, lambda: [when(eng, g & (STRIPS - 1), p, lambda: both(p)) for p in phases])
    else:
        for p in phases:
            if step.part == 0:
                when(eng, g, p, lambda: body(p, "A", x_image))
                when(eng, g, p + STRIPS, lambda: both(p))
            else:
                when(eng, g, p + TOTAL, lambda: body(p, "B", x1_image))


def window_attention_layers(nc, x, qkv_w, qkv_b, proj_w, proj_b, bias_rev, mask, ident_in, group_in, out):
    with ExitStack() as ctx:
        ctx.enter_context(nc.allow_non_contiguous_dma("small loads of biases and the relative bias table"))

        def sb(name, shape):
            return ctx.enter_context(nc.sbuf_tensor(name, shape, F32))

        def sem(name):
            return ctx.enter_context(nc.semaphore(name))

        score_banks = ctx.enter_context(nc.psum_tensor("score_banks", [128, HEADS, 512], F32))
        q_bank, k_bank = [ctx.enter_context(nc.psum_tensor(f"{b}_bank", [128, 512], F32)) for b in ("q", "k")]
        o_banks = ctx.enter_context(nc.psum_tensor("o_banks", [128, 2, 512], F32))
        y_bank = k_bank
        v_bank, ot_bank = o_banks[:, 0, :], o_banks[:, 1, :]
        o_groups = o_banks[:, :, 0:HEADS * 2 * VW].rearrange("p b (g v) -> p b g v", v=VW)
        swap_bank = score_banks[:, 2, :]
        stat_col = {"A": q_bank[:, 508:509], "B": q_bank[:, 509:510]}

        ident = sb("ident", [128, 128])
        group_avg = sb("group_avg", [128, 128])
        w_qkv = {s: sb(f"w_qkv_{s}", [CH, 3 * CH]) for s in "AB"}
        w_proj = {s: sb(f"w_proj_{s}", [CH, CH]) for s in "AB"}
        b_qkv = {s: sb(f"b_qkv_{s}", [CH, 3]) for s in "AB"}
        b_proj = {s: sb(f"b_proj_{s}", [CH, 1]) for s in "AB"}
        b_q_scaled = {s: sb(f"b_q_scaled_{s}", [CH, 1]) for s in "AB"}
        mask_tab = sb("mask_tab", [128, 2 * PAIRS * N])
        bias_tab = sb("bias_tab", [128, HEADS * N])
        minus_half = sb("minus_half", [128, 1])
        eps = sb("eps", [128, 1])
        idle_dve = {s: sb(f"idle_dve_{s}", [128, 1]) for s in "AB"}
        idle_after = {s: sb(f"idle_after_{s}", [128, 1]) for s in "AB"}
        zero = sb("zero", [128, 1])

        xr = sb("xr", [128, RING * IMG])
        x1r = sb("x1r", [128, RING * IMG])
        x_in = [sb(f"x_in{i}", [PT, JT * CH]) for i in range(2)]
        xn = [sb(f"xn{i}", [128, WINS * WPAD]) for i in range(2)]
        q_t = sb("q_t", [128, TOK])
        k_t = sb("k_t", [128, TOK])
        v_bd = [sb(f"v_bd{i}", [128, 2, 2, HEADS, 2, VW]) for i in range(2)]
        logits = sb("logits", [128, HEADS, PAIRS, N])
        neg_max = sb("neg_max", [128, HEADS, PAIRS])
        probs = sb("probs", [128, HEADS, PAIRS, WPAD])
        probs_t = sb("probs_t", [128, 2, 2, 2, 2, N])
        sums = sb("sums", [128, 2, HEADS * 2])
        inv_sums = sb("inv_sums", [128, 2, HEADS * 2])
        o_sb = sb("o_sb", [128, PAIRS, CH])
        o_t = sb("o_t", [128, TOK])
        y_t = sb("y_t", [128, TOK])
        out_st = sb("out_st", [PT, JT * CH])
        bn = {s: sb(f"bn_{s}", [128, STRIPS * 6]) for s in "AB"}
        chan = {s: sb(f"chan_{s}", [128, 2]) for s in "AB"}
        gmean = {s: sb(f"gmean_{s}", [128, 1]) for s in "AB"}
        dev = {s: sb(f"dev_{s}", [128, 1]) for s in "AB"}
        dev2 = {s: sb(f"dev2_{s}", [128, 1]) for s in "AB"}
        spread = {s: sb(f"spread_{s}", [128, 1]) for s in "AB"}
        gvar = {s: sb(f"gvar_{s}", [128, 1]) for s in "AB"}
        grstd = {s: sb(f"grstd_{s}", [128, 1]) for s in "AB"}
        cur_mean = {s: sb(f"cur_mean_{s}", [128, 1]) for s in "AB"}
        cur_rstd = {s: sb(f"cur_rstd_{s}", [128, 1]) for s in "AB"}

        consts_in = sem("consts_in")
        bias_in = sem("bias_in")
        buffers_set = sem("buffers_set")
        banks_set = sem("banks_set")
        x_loaded = [sem(f"x_loaded{i}") for i in range(2)]
        x_swapped = sem("x_swapped")
        x_stored = sem("x_stored")
        x_padded = sem("x_padded")
        x1_padded = sem("x1_padded")
        norm_done = sem("norm_done")
        q_done, k_done, v_done = sem("q_done"), sem("k_done"), sem("v_done")
        q_copied, k_copied = sem("q_copied"), sem("k_copied")
        v_copied0, v_copied1 = sem("v_copied0"), sem("v_copied1")
        scores_done = sem("scores_done")
        biased = sem("biased")
        max_done = sem("max_done")
        shifted = sem("shifted")
        exp_done = sem("exp_done")
        pt_done, pt_copied = sem("pt_done"), sem("pt_copied")
        o_done = sem("o_done")
        sums_safe, sums_inverted = sem("sums_safe"), sem("sums_inverted")
        o_scaled = sem("o_scaled")
        ot_done, ot_copied = sem("ot_done"), sem("ot_copied")
        y_done, y_taken = sem("y_done"), sem("y_taken")
        x1_written = sem("x1_written")
        y_swapped, y_staged, y_stored = sem("y_swapped"), sem("y_staged"), sem("y_stored")
        bn_done = {s: sem(f"bn_done_{s}") for s in "AB"}
        chan_done = {s: sem(f"chan_done_{s}") for s in "AB"}
        gmean_mm = {s: sem(f"gmean_mm_{s}") for s in "AB"}
        gmean_out = {s: sem(f"gmean_out_{s}") for s in "AB"}
        spread_out = {s: sem(f"spread_out_{s}") for s in "AB"}
        gvar_mm = {s: sem(f"gvar_mm_{s}") for s in "AB"}
        gvar_out = {s: sem(f"gvar_out_{s}") for s in "AB"}
        pool_step = sem("pool_step")
        stats_cur = {s: sem(f"stats_cur_{s}") for s in "AB"}

        def stat_matmul(pe, s, image):
            at_least(pe, chan_done[s], image + 1)
            nc.tensor.matmul(stat_col[s], group_avg[:, :], chan[s][:, 0:1], start=True, stop=True)\
                .then_inc(gmean_mm[s], 1)

        def spread_matmul(pe, s, image):
            at_least(pe, spread_out[s], image + 1)
            nc.tensor.matmul(stat_col[s], group_avg[:, :], spread[s][:, :], start=True, stop=True)\
                .then_inc(gvar_mm[s], 1)

        def mean_copy(act, s, image):
            at_least(act, gmean_mm[s], image + 1)
            nc.scalar.copy(gmean[s][:, :], stat_col[s]).then_inc(gmean_out[s], 1)

        def var_copy(act, s, image):
            at_least(act, gvar_mm[s], image + 1)
            nc.scalar.activation(gvar[s][:, :], stat_col[s], ACT.Identity, bias=eps[:, :]).then_inc(gvar_out[s], 1)

        def stat_copy(act):
            return lambda phase, s, image: (mean_copy if phase == MEAN else var_copy)(act, s, image)

        def stat_product(pe):
            return lambda phase, s, image: (stat_matmul if phase == MEAN else spread_matmul)(pe, s, image)

        def v_half(step, a):
            src = o_banks[a * WPAD:(a + 1) * WPAD, 0, :].rearrange("p (g h d) -> p g h d", g=4, h=HEADS)
            dst = v_bd[step.parity][a * WPAD:(a + 1) * WPAD].rearrange("p b w h a v -> p (b w) h a v")
            return dst[:, :, :, a, 0:HD], src

        def slot_of(c, parity=0):
            return c % 2 if isinstance(c, int) else parity

        block = ctx.enter_context(nc.Block())

        @block.sync
        def _(sp):
            def chunk(images, k):
                at = k * (TOK * CH)
                return bass.AP(images.tensor, at if isinstance(k, int) else sp.snap(at),
                               [[JT * CH, PT], [1, JT * CH]])

            def load(c, k, slot, swapped):
                src = chunk(x, k)
                if not isinstance(swapped, int):
                    swapped = sp.snap(swapped)
                at_least(sp, x_swapped, swapped)
                sp.dma_start(x_in[slot][:, :], src).then_inc(x_loaded[slot], 16)

            for slot in range(2):
                load(slot, slot, slot, 0)
            sp.dma_start(ident[:, :], ident_in).then_inc(consts_in, 16)
            sp.dma_start(group_avg[:, :], group_in).then_inc(consts_in, 16)
            for s in "AB":
                sp.dma_start(w_qkv[s][:, :], qkv_w[s]).then_inc(consts_in, 16)
                sp.dma_start(w_proj[s][:, :], proj_w[s]).then_inc(consts_in, 16)
                sp.dma_start(b_qkv[s][:, :], qkv_b[s].rearrange("(t p) -> p t", p=CH)).then_inc(consts_in, 16)
                sp.dma_start(b_proj[s][:, :], proj_b[s].rearrange("(p o) -> p o", o=1)).then_inc(consts_in, 16)
            sp.dma_start(mask_tab[:, :], mask).then_inc(consts_in, 16)
            def relative_bias(q):
                first = (WS - 1 - q // WS) * TABLE_SIDE + WS - 1 - q % WS
                src = bass.AP(bias_rev.tensor, bias_rev.offset + first,
                              [[TABLE_SIDE ** 2, 1], [TABLE_SIDE ** 2, HEADS], [TABLE_SIDE, WS], [1, WS]])
                dst = bias_tab[q:q + 1, :].rearrange("p (h a b) -> p h a b", h=HEADS, a=WS)
                sp.dma_start(dst, src).then_inc(bias_in, 16)

            for c in range(2, LEAD + 1):
                load(c, c, c % 2, c - 1)
                if c == 2:
                    sp.wait_ge(buffers_set, 1)
                for q in range((c - 2) * 4, min((c - 1) * 4, N)):
                    relative_bias(q)
            sp.wait_ge(bias_in, N * 16)
            sp.dma_start(bias_tab[WPAD:WPAD + N, :], bias_tab[0:N, :]).then_inc(bias_in, 16)

            def step(before, prev, cur, nxt, after):
                if cur is not None and cur.stream == "A":
                    c = cur.strip + LEAD + 1
                    if isinstance(c, int):
                        if c < TOTAL + LEAD:
                            paired = c < LAG + LEAD
                            load(c, c % TOTAL, c % 2 if paired else 0, c - 1 if paired else c)
                    elif cur.part == 0:
                        load(c, c, 1 - cur.parity, c - 1)
                    else:
                        load(c, c % TOTAL, 0, c)
                if before is not None and before.stream == "B":
                    m = before.strip
                    at_least(sp, y_staged, m + 1)
                    sp.dma_start(chunk(out, m), out_st[:, :]).then_inc(y_stored, 16)
            walk(sp, step)
            sp.wait_ge(y_stored, TOTAL * 16)

        @block.gpsimd
        def _(pool):
            nc.gpsimd.memset(zero[:, :], 0.0)
            nc.gpsimd.memset(minus_half[:, :], -0.5).then_inc(pool_step, 1)
            pool.wait_ge(pool_step, 1)

            def pad_image(ring, img, done, to_low):
                off = img % RING * IMG
                own = SHIFT if to_low else 0
                for r0, c0, n, width, dr, dc in ((own, 0, SIDE, SHIFT, 0, 1), (0, own, SHIFT, SIDE, 1, 0),
                                                 (0, 0, SHIFT, SHIFT, 1, 1)):
                    first = rows(ring, off + r0 * PITCH, c0, width, n)
                    second = rows(ring, off + (r0 + dr * SIDE) * PITCH, c0 + dc * SIDE, width, n)
                    dst, src = (first, second) if to_low else (second, first)
                    nc.gpsimd.tensor_copy(dst, src).then_inc(done, 1)

            def spread_of(s, img, before):
                pool.wait_ge(gmean_out[s], img + 1)
                nc.gpsimd.tensor_tensor(dev[s][:, :], chan[s][:, 0:1], gmean[s][:, :], ALU.subtract)\
                    .then_inc(pool_step, 1)
                pool.wait_ge(pool_step, before + 1)
                nc.gpsimd.tensor_tensor(dev2[s][:, :], dev[s][:, :], dev[s][:, :], ALU.mult)\
                    .then_inc(pool_step, 1)
                pool.wait_ge(pool_step, before + 2)
                nc.gpsimd.tensor_tensor(spread[s][:, :], dev2[s][:, :], chan[s][:, 1:2], ALU.add)\
                    .then_inc(spread_out[s], 1)

            def invert(s, img, before):
                pool.wait_ge(gvar_out[s], img + 1)
                nc.gpsimd.tensor_tensor(grstd[s][:, :], gvar[s][:, :], minus_half[:, :], ALU.pow)\
                    .then_inc(pool_step, 1)
                pool.wait_ge(pool_step, before + 1)

            def publish(s, normed):
                for to, of in ((cur_mean[s], gmean[s]), (cur_rstd[s], grstd[s])):
                    at_least(pool, norm_done, normed)
                    nc.gpsimd.tensor_tensor(to[:, :], of[:, :], zero[:, :], ALU.add).then_inc(stats_cur[s], 1)

            pool.wait_ge(x_stored, STRIPS)
            pad_image(xr, 0, x_padded, False)
            spread_of("A", 0, 1)
            invert("A", 0, 3)
            publish("A", 0)
            pool.wait_ge(x_stored, 2 * STRIPS)
            pad_image(xr, 1, x_padded, False)

            def image(i, before, a_normed, b_normed):
                if b_normed is None:
                    spread_of("A", i + 1, before)
                    invert("A", i + 1, before + 2)
                else:
                    pool.wait_ge(x1_written, i * STRIPS)
                    pad_image(x1r, i - 1, x1_padded, True)
                    spread_of("A", i + 1, before)
                    spread_of("B", i - 1, before + 2)
                    invert("A", i + 1, before + 4)
                    invert("B", i - 1, before + 5)
                publish("A", a_normed)
                if b_normed is not None:
                    publish("B", b_normed)
                pool.wait_ge(x_stored, (i + 3) * STRIPS)
                pad_image(xr, i + 2, x_padded, False)

            image(0, 4, STRIPS, None)
            image(1, 7, 2 * STRIPS, 0)
            with pool.Fori(2, IMAGES) as i:
                image(i, i * 6 + 1, i * 16 - 1, i * 16)
            pool.wait_ge(x1_written, TOTAL)
            pad_image(x1r, IMAGES - 1, x1_padded, True)
            spread_of("B", IMAGES - 1, IMAGES * 6 + 1)
            invert("B", IMAGES - 1, IMAGES * 6 + 3)
            publish("B", STEPS - STRIPS)

        @block.scalar
        def _(act):
            act.wait_ge(consts_in, 16 * 11)
            act.wait_ge(buffers_set, 2)
            act.wait_ge(banks_set, 1)

            def place_of(c):
                dst = rows(xr, ring_at(act, c), 0)
                return bass.AP(dst.tensor, dst.offset, [dst.ap[0], [PITCH, WS], [JT, SIDE // JT], [1, JT]])

            def store_chunk(c, dst):
                src = swap_bank[:, 0:TOK].rearrange("p (j r q) -> p r q j", j=JT, r=WS)
                at_least(act, x_swapped, c + 1)
                nc.scalar.copy(dst, src).then_inc(x_stored, 1)

            def exponentials(st, k):
                at_least(act, shifted, st.n * 2 + k + 1)
                heads = slice(2 * HP_ORDER[k], 2 * HP_ORDER[k] + 2)
                nc.scalar.activation(
                    probs[:, heads].rearrange("p h j k -> p (h j) k")[:, :, 0:N],
                    logits[:, heads].rearrange("p h j k -> p (h j) k"), ACT.Exp).then_inc(exp_done, 1)

            with act.Fori(0, STRIPS) as c:
                store_chunk(c, place_of(c))
            with act.Fori(STRIPS, LEAD) as c:
                when(act, c, STRIPS + MEAN, lambda: mean_copy(act, "A", 0))
                when(act, c, STRIPS + VAR, lambda: var_copy(act, "A", 0))
                store_chunk(c, place_of(c))

            def step(before, prev, cur, nxt, after):
                if cur is not None and cur.stream == "A":
                    chunk_place = place_of(cur.strip + LEAD)
                if nxt is not None:
                    s = nxt.stream
                    at_least(act, q_done, nxt.n + 1)
                    nc.scalar.activation(q_t[:, :], q_bank[:, 0:TOK], ACT.Identity,
                                         bias=b_q_scaled[s][:, :], scale=SCALE[s]).then_inc(q_copied, 1)
                    at_least(act, k_done, nxt.n + 1)
                    nc.scalar.activation(k_t[:, :], k_bank[:, 0:TOK], ACT.Identity,
                                         bias=b_qkv[s][:, 1:2]).then_inc(k_copied, 1)
                if cur is not None:
                    exponentials(cur, 1)
                if cur is not None and cur.stream == "A":
                    store_chunk(cur.strip + LEAD, chunk_place)
                if before is not None and before.stream == "B":
                    m = before.strip
                    at_least(act, y_stored, m * 16)
                    at_least(act, y_swapped, m + 1)
                    nc.scalar.copy(out_st[:, :], score_banks[0:PT, 2, :]).then_inc(y_staged, 1)
                if nxt is not None:
                    at_least(act, v_done, nxt.n + 1)
                    nc.scalar.copy(*v_half(nxt, 0)).then_inc(v_copied0, 1)
                if prev is not None:
                    at_least(act, ot_done, prev.n + 1)
                    src = ot_bank.rearrange("p (w q) -> p w q", q=WPAD)[:, :, 0:N]\
                        .rearrange("p w (i j) -> p w i j", j=WS)
                    dst = o_t[:, :].rearrange("p (i w j) -> p w i j", w=WINS, j=WS)
                    nc.scalar.activation(dst, src, ACT.Identity, bias=b_qkv[prev.stream][:, 2:3])\
                        .then_inc(ot_copied, 1)
                if cur is not None:
                    for k, hp in enumerate(HP_ORDER):
                        at_least(act, pt_done, cur.n * 2 + k + 1)
                        src = score_banks[:, hp, :].rearrange("p (b q) -> p b q", q=WPAD)[:, :, 0:N]
                        dst = probs_t[:, hp].rearrange("p a b w q -> p (a b w) q")
                        nc.scalar.copy(dst, src).then_inc(pt_copied, 1)
                at_phase(act, cur, (MEAN, VAR), stat_copy(act), order="BA")
                if nxt is not None:
                    exponentials(nxt, 0)
            walk(act, step)

        @block.vector
        def _(dve):
            for buf in (bias_tab, probs, xn[0], xn[1], v_bd[0]):
                shape = " ".join("abcdefg"[:len(buf.shape) - 1])
                nc.vector.memset(buf[:].rearrange(f"p {shape} -> p ({shape})"), 0.0)
            nc.vector.memset(v_bd[1][:].rearrange("p a b c d e -> p (a b c d e)"), 0.0).then_inc(buffers_set, 1)
            dve.wait_ge(buffers_set, 1)
            nc.vector.memset(eps[:, :], GN_EPS)
            for i in range(2):
                for a in range(2):
                    ones = v_bd[i][a * WPAD:(a + 1) * WPAD].rearrange("p b w h a v -> p (b w h) a v")
                    nc.vector.memset(ones[:, :, a, HD:VW], 1.0)
            dve.wait_ge(consts_in, 16 * 11)
            nc.vector.tensor_scalar(b_q_scaled["A"][:, :], b_qkv["A"][:, 0:1], SCALE["A"], None, ALU.mult)
            nc.vector.tensor_scalar(b_q_scaled["B"][:, :], b_qkv["B"][:, 0:1], SCALE["B"], None, ALU.mult)\
                .then_inc(buffers_set, 1)
            for b in (q_bank[:, :], k_bank[:, :], v_bank, ot_bank):
                nc.vector.memset(b, 0.0)
            nc.vector.memset(score_banks[:, :, :].rearrange("p h c -> p (h c)"), 0.0).then_inc(banks_set, 1)

            def chunk_stats(c):
                at_least(dve, x_stored, c + 1)
                nc.vector.bn_stats(bn["A"][:, bass.ds((c & 7) * 6, 6)], rows(xr, ring_at(dve, c), 0))\
                    .then_inc(bn_done["A"], 1)

            def channel_stats(s, count, done):
                at_least(dve, bn_done[s] if s == "A" else x1_written, count)
                nc.vector.memset(idle_dve[s][:, :], 0.0)
                nc.vector.bn_aggr(chan[s][:, :], bn[s][:, :]).then_inc(chan_done[s], 1)
                at_least(dve, chan_done[s], done)
                nc.vector.memset(idle_after[s][:, :], 0.0)

            for first in (0, STRIPS):
                with dve.Fori(first, first + STRIPS) as c:
                    chunk_stats(c)
                if first == 0:
                    channel_stats("A", STRIPS, 1)
            dve.wait_ge(stats_cur["A"], 2)
            channel_stats("A", 2 * STRIPS, 2)

            def normalise(st):
                s, strip = st.stream, st.strip
                at_least(dve, v_done, st.n - 1)
                img = strip >> 3
                at_least(dve, stats_cur[s], img * 2 + 2)
                at_least(dve, x_padded if s == "A" else x1_padded, img * 3 + 3)
                off = ring_at(dve, strip)
                start = SHIFT * PITCH + SHIFT if s == "A" else 0
                v = rows(xr if s == "A" else x1r, off + start, 0)
                src = bass.AP(v.tensor, v.offset, [v.ap[0], [WS, WINS], [PITCH, WS], [1, WS]])
                dst = xn[st.parity][:, :].rearrange("p (w q) -> p w q", q=WPAD)[:, :, 0:N]\
                    .rearrange("p w (i j) -> p w i j", j=WS)
                nc.vector.tensor_scalar(dst, src, cur_mean[s][:, :], cur_rstd[s][:, :],
                                        ALU.subtract, ALU.mult).then_inc(norm_done, 1)

            def of_heads(hp):
                return slice(2 * hp, 2 * hp + 2)

            def in_bank(hp):
                return score_banks[:, of_heads(hp), 0:PAIRS * N]

            def add_table(st, k):
                hp = HP_ORDER[k]
                n = st.n * 2 + k + 1
                if st.stream == "A":
                    last = (st.strip & 7) + 1 >> 3
                    table = mask_tab[:, bass.ds(last * (PAIRS * N), PAIRS * N)]
                    table = bass.AP(table.tensor, table.offset, [table.ap[0], [0, 2], [1, PAIRS * N]])
                    at_least(dve, scores_done, n)
                    nc.vector.tensor_tensor(logits[:, of_heads(hp)].rearrange("p h j k -> p h (j k)"),
                                            in_bank(hp), table, ALU.add).then_inc(biased, 1)
                else:
                    if k == 0:
                        at_least(dve, bias_in, (N + 1) * 16)
                    table = bias_tab[:, 2 * hp * N:(2 * hp + 2) * N]
                    table = bass.AP(table.tensor, table.offset, [table.ap[0], [N, 2], [0, PAIRS], [1, N]])
                    at_least(dve, scores_done, n)
                    nc.vector.tensor_tensor(logits[:, of_heads(hp)],
                                            in_bank(hp).rearrange("p h (j k) -> p h j k", k=N), table, ALU.add)\
                        .then_inc(biased, 1)

            def row_max(st, k):
                n = st.n * 2 + k + 1
                at_least(dve, biased, n)
                nc.vector.tensor_reduce(neg_max[:, of_heads(HP_ORDER[k])], logits[:, of_heads(HP_ORDER[k])], AX.X, ALU.max,
                                        negate=True).then_inc(max_done, 1)

            def subtract_max(st, k):
                n = st.n * 2 + k + 1
                at_least(dve, max_done, n)
                top = neg_max[:, of_heads(HP_ORDER[k])]
                top = bass.AP(top.tensor, top.offset, [top.ap[0], [PAIRS, 2], [1, PAIRS], [0, N]])
                nc.vector.tensor_tensor(logits[:, of_heads(HP_ORDER[k])], logits[:, of_heads(HP_ORDER[k])], top, ALU.add)\
                    .then_inc(shifted, 1)

            def add_residual(st):
                s = st.stream
                off = ring_at(dve, st.strip)
                at_least(dve, y_done, st.n + 1)
                y = y_bank[:, 0:TOK].rearrange("p (i c) -> p i c", i=WS)
                if s == "A":
                    place = off + SHIFT * PITCH
                    nc.vector.scalar_tensor_tensor(
                        rows(x1r, place, SHIFT), y, b_proj[s][:, :], rows(xr, place, SHIFT),
                        ALU.add, ALU.add).then_inc(y_taken, 1)
                else:
                    nc.vector.scalar_tensor_tensor(
                        y_t[:, :].rearrange("p (i c) -> p i c", i=WS), y, b_proj[s][:, :],
                        rows(x1r, off, 0), ALU.add, ALU.add).then_inc(y_taken, 1)

            def x1_stats(st):
                at_least(dve, y_taken, st.n + 1)
                nc.vector.bn_stats(bn["B"][:, bass.ds((st.strip & 7) * 6, 6)],
                                   rows(x1r, ring_at(dve, st.strip) + SHIFT * PITCH, SHIFT)).then_inc(x1_written, 1)

            def clamp_sums(st):
                at_least(dve, o_done, st.n + 1)
                nc.vector.tensor_scalar(sums[:, :, :], o_groups[:, :, :, HD], 0.5, None, ALU.max)\
                    .then_inc(sums_safe, 1)

            def scale_outputs(st):
                at_least(dve, sums_safe, st.n + 1)
                nc.vector.reciprocal(inv_sums[:, :, :], sums[:, :, :]).then_inc(sums_inverted, 1)
                at_least(dve, sums_inverted, st.n + 1)
                inv = inv_sums[:, :, :]
                inv = bass.AP(inv.tensor, inv.offset, [inv.ap[0], [2 * HEADS, 2], [1, 2 * HEADS], [0, HD]])
                nc.vector.tensor_tensor(
                    o_sb[:, :, :].rearrange("p (b a) (h d) -> p b (a h) d", b=2, h=HEADS),
                    o_groups[:, :, :, 0:HD], inv, ALU.mult).then_inc(o_scaled, 1)

            def step(before, prev, cur, nxt, after):
                if nxt is not None:
                    at_least(dve, v_done, nxt.n + 1)
                    nc.vector.tensor_copy(*v_half(nxt, 1)).then_inc(v_copied1, 1)
                chunk = cur.strip + LEAD if cur is not None and cur.stream == "A" else None
                if nxt is not None:
                    add_table(nxt, 0)
                if after is not None:
                    normalise(after)
                if nxt is not None:
                    row_max(nxt, 0)
                if nxt is not None:
                    subtract_max(nxt, 0)
                if prev is not None:
                    add_residual(prev)
                if cur is not None:
                    clamp_sums(cur)
                if prev is not None and prev.stream == "A":
                    x1_stats(prev)
                if cur is not None:
                    scale_outputs(cur)
                if nxt is not None:
                    add_table(nxt, 1)
                at_phase(dve, cur, (CHAN,), lambda phase, s, image: channel_stats(
                    s, (image + 1) * STRIPS, image + 1), first_x=STRIPS)
                if chunk is not None:
                    chunk_stats(chunk)
                if nxt is not None:
                    row_max(nxt, 1)
                    subtract_max(nxt, 1)

            walk(dve, step)

        @block.tensor
        def _(pe):
            pe.wait_ge(consts_in, 16 * 11)
            pe.wait_ge(banks_set, 1)
            pe.wait_ge(buffers_set, 2)

            def swap_chunk(c, slot, loaded):
                at_least(pe, x_loaded[slot], loaded)
                for j in range(JT):
                    last = nc.tensor.transpose(swap_bank[:, j * PT:(j + 1) * PT],
                                               x_in[slot][:, j * CH:(j + 1) * CH], ident[0:PT, 0:PT])
                last.then_inc(x_swapped, 1)

            def first_chunks(half_c):
                for slot in range(2):
                    c = half_c * 2 + slot
                    at_least(pe, x_stored, c)
                    if not isinstance(c, int):
                        when(pe, c, STRIPS + MEAN, lambda: stat_matmul(pe, "A", 0))
                        when(pe, c, STRIPS + VAR, lambda: spread_matmul(pe, "A", 0))
                    swap_chunk(c, slot, half_c * 16 + 16)

            first_chunks(0)
            with pe.Fori(1, LEAD // 2) as half_c:
                first_chunks(half_c)
            pe.wait_ge(x_stored, LEAD)

            def scores(hp):
                for win in range(WINS):
                    j, half = place(win)
                    for h in (2 * hp, 2 * hp + 1):
                        last = nc.tensor.matmul(
                            score_banks[half * WPAD:half * WPAD + N, h, j * N:(j + 1) * N],
                            q_t[h * HD:(h + 1) * HD, win * N:(win + 1) * N],
                            k_t[h * HD:(h + 1) * HD, win * N:(win + 1) * N], start=True, stop=True)
                last.then_inc(scores_done, 1)

            def step(before, prev, cur, nxt, after):
                if nxt is not None:
                    w, tokens = w_qkv[nxt.stream], xn[nxt.parity]
                    moving = tokens[:, :].rearrange("p (w q) -> p w q", q=WPAD)[:, :, 0:N]
                    at_least(pe, norm_done, nxt.n + 1)
                    at_least(pe, q_copied, nxt.n)
                    if cur is not None:
                        at_least(pe, exp_done, cur.n * 2 + 1)
                    nc.tensor.matmul(q_bank[:, 0:TOK], w[:, 0:CH], moving, start=True, stop=True)\
                        .then_inc(q_done, 1)
                    at_least(pe, y_taken, nxt.n - 2)
                    nc.tensor.matmul(k_bank[:, 0:TOK], w[:, CH:2 * CH], moving, start=True, stop=True)\
                        .then_inc(k_done, 1)
                if cur is not None:
                    at_least(pe, shifted, cur.n * 2 + 1)
                if cur is not None and cur.stream == "A":
                    c = cur.strip + LEAD
                    if cur.part == 0:
                        slot = cur.parity
                        loaded = ((c >> 1) + 1) * 16
                    else:
                        slot = 0
                        loaded = (c - (LAG + LEAD) // 2 + 1) * 16
                    swap_chunk(c, slot, loaded)
                if before is not None and before.stream == "B":
                    at_least(pe, y_taken, before.n + 1)
                    for j in range(JT):
                        last = nc.tensor.transpose(score_banks[0:PT, 2, j * CH:(j + 1) * CH],
                                                   y_t[:, j::JT], ident[:, :])
                    last.then_inc(y_swapped, 1)
                if nxt is not None:
                    at_least(pe, o_scaled, nxt.n - 1)
                    if prev is None:
                        at_least(pe, v_copied0, nxt.n)
                        at_least(pe, v_copied1, nxt.n)
                    for b in range(WINS // 2):
                        last = nc.tensor.matmul(o_banks[:, 0, b * CH:(b + 1) * CH],
                                                tokens[:, b * 2 * WPAD:(b + 1) * 2 * WPAD],
                                                w[:, 2 * CH:3 * CH], start=True, stop=True)
                    last.then_inc(v_done, 1)
                if prev is not None:
                    at_least(pe, o_scaled, prev.n + 1)
                    for j in range(PAIRS):
                        first = (4 * (j // 2) + j % 2) * WPAD
                        dst = o_banks[:, 1, first:first + 3 * WPAD]
                        dst = bass.AP(dst.tensor, dst.offset, [dst.ap[0], [2 * WPAD, 2], [1, WPAD]])
                        last = nc.tensor.transpose(dst, o_sb[:, j, :], ident[:, :])
                    last.then_inc(ot_done, 1)
                if cur is not None:
                    at_least(pe, shifted, cur.n * 2 + 2)
                    for k, hp in enumerate(HP_ORDER):
                        at_least(pe, exp_done, cur.n * 2 + k + 1)
                        for h2 in range(2):
                            for pp in range(2):
                                b = h2 * 2 + pp
                                last = nc.tensor.transpose(
                                    score_banks[:, hp, b * 128:(b + 1) * 128],
                                    probs[:, 2 * hp + h2, 2 * pp:2 * pp + 2, :].rearrange("p j k -> p (j k)"),
                                    ident[:, :])
                        last.then_inc(pt_done, 1)
                if nxt is not None:
                    at_least(pe, q_copied, nxt.n + 1)
                    at_least(pe, k_copied, nxt.n + 1)
                    if cur is not None and cur.stream == "A":
                        at_least(pe, x_stored, cur.strip + LEAD + 1)
                    if before is not None and before.stream == "B":
                        at_least(pe, y_staged, before.strip + 1)
                    scores(HP_ORDER[0])
                at_phase(pe, cur, (MEAN, VAR), stat_product(pe))
                if prev is not None:
                    at_least(pe, ot_copied, prev.n + 1)
                    nc.tensor.matmul(y_bank[:, 0:TOK], w_proj[prev.stream][:, :], o_t[:, :],
                                     start=True, stop=True).then_inc(y_done, 1)
                if cur is not None:
                    at_least(pe, pt_copied, cur.n * 2 + 2)
                    if nxt is not None:
                        at_least(pe, v_copied0, nxt.n + 1)
                        at_least(pe, v_copied1, nxt.n + 1)
                    for pp in range(2):
                        for h in range(HEADS):
                            for half in range(2):
                                of_pairs = o_groups[half * WPAD:half * WPAD + N, pp, h::HEADS, :]
                                last = nc.tensor.matmul(
                                    of_pairs, probs_t[:, h // 2, h % 2, pp, half, :],
                                    v_bd[cur.parity][:, pp, half, h].rearrange("p a v -> p (a v)"),
                                    start=True, stop=True)
                    last.then_inc(o_done, 1)
                if nxt is not None:
                    at_least(pe, pt_copied, nxt.n * 2)
                    scores(HP_ORDER[1])
            walk(pe, step)


def kernel(x, L0_conv_qkv_w, L0_conv_qkv_b, L0_conv_proj_w, L0_conv_proj_b,
           L1_conv_qkv_w, L1_conv_qkv_b, L1_conv_proj_w, L1_conv_proj_b, L1_conv_bias_table):
    import numpy as np
    import concourse.bacc as bacc
    from concourse.bass_utils import run_bass_kernel_spmd

    region = np.zeros((SIDE, SIDE), np.int32)
    cuts = (slice(0, -WS), slice(-WS, -SHIFT), slice(-SHIFT, None))
    for a, rs in enumerate(cuts):
        for b, cs in enumerate(cuts):
            region[rs, cs] = 3 * a + b
    mask = np.zeros((128, 2, PAIRS, N), np.float32)
    for last in range(2):
        for win in range(WINS):
            r = region[(STRIPS - 1) * last * WS:((STRIPS - 1) * last + 1) * WS,
                       win * WS:(win + 1) * WS].reshape(-1)
            pair, half = place(win)
            q = half * WPAD
            mask[q:q + N, last, pair] = np.where(r[:, None] != r[None, :], -1e9, 0.0)

    feeds = {
        "x": x, "mask": mask.reshape(128, -1), "ident": np.eye(128, dtype=np.float32),
        "group": np.kron(np.eye(GROUPS), np.full((CH // GROUPS,) * 2, GROUPS / CH)).astype(np.float32),
        "bias_rev": np.ascontiguousarray(np.asarray(L1_conv_bias_table)[::-1].T),
        "qkv_w_A": L0_conv_qkv_w, "qkv_b_A": L0_conv_qkv_b, "proj_w_A": L0_conv_proj_w, "proj_b_A": L0_conv_proj_b,
        "qkv_w_B": L1_conv_qkv_w, "qkv_b_B": L1_conv_qkv_b, "proj_w_B": L1_conv_proj_w, "proj_b_B": L1_conv_proj_b,
    }
    feeds = {k: np.ascontiguousarray(v) for k, v in feeds.items()}
    nc = bacc.Bacc("TRN2", target_bir_lowering=False, num_devices=1)
    d = {k: nc.dram_tensor(f"in_{k}", v.shape, mybir.dt.from_np(v.dtype), kind="ExternalInput").ap()
         for k, v in feeds.items()}
    out = nc.dram_tensor("out", feeds["x"].shape, F32, kind="ExternalOutput").ap()
    window_attention_layers(
        nc, d["x"], {s: d[f"qkv_w_{s}"] for s in "AB"}, {s: d[f"qkv_b_{s}"] for s in "AB"},
        {s: d[f"proj_w_{s}"] for s in "AB"}, {s: d[f"proj_b_{s}"] for s in "AB"},
        d["bias_rev"], d["mask"], d["ident"], d["group"], out)
    r = run_bass_kernel_spmd(nc, [{f"in_{k}": v for k, v in feeds.items()}], core_ids=[0])
    return r.results[0]["out"]
```

```python
from contextlib import ExitStack

import concourse.bass as bass
from concourse import mybir

F32 = mybir.dt.float32
F32R = mybir.dt.float32r
ACT = mybir.ActivationFunctionType
ALU = mybir.AluOpType
AX = mybir.AxisListType

IMAGES, SIDE, CH = 64, 56, 128
WS, SHIFT, HEADS, GROUPS = 7, 3, 4, 32
HD = CH // HEADS
N = WS * WS
WPAD = 64
WINS = SIDE // WS
PAIRS = WINS // 2
STRIPS = SIDE // WS
TOK = WINS * N
PITCH = SIDE + SHIFT
ROWS_STRIP = WS * PITCH
IMG = PITCH * PITCH
RING = 3
TOTAL = IMAGES * STRIPS
LAG = 2 * STRIPS
LEAD = 2 * STRIPS
JT = 4
PT = TOK // JT
VW = HD + 1
GN_EPS = 1e-5
TABLE_SIDE = 2 * WS - 1
SCALE = {"A": float(CH) ** -0.5, "B": float(HD) ** -0.5}

STEPS = 2 * TOTAL
ALONE = LAG
HP_ORDER = (1, 0)
ROUND = 4
SCHEDULE = [(-2, 2, False), (2, ALONE - 2, True), (ALONE - 2, ALONE + 6, False),
            (ALONE + 6, STEPS - ALONE - 2, True), (STEPS - ALONE - 2, STEPS - ALONE + 2, False),
            (STEPS - ALONE + 2, STEPS - 2, True), (STEPS - 2, STEPS + 2, False)]


def place(win):
    pp, w, a = win // 4, win // 2 % 2, win % 2
    return 2 * pp + a, w


class Step:

    def __init__(self, n, stream, strip, parity, part, odd):
        self.n, self.stream, self.strip = n, stream, strip
        self.parity = parity
        self.part = part
        self.odd = odd
        self.g = strip if stream == "A" else strip + LAG
        self.leads = stream == "A" or part == 2


def step_at(u):
    if u < 0 or u >= STEPS:
        return None
    if u < ALONE:
        return Step(u, "A", u, u % 2, 0, u % 2)
    if u >= STEPS - ALONE:
        return Step(u, "B", u - TOTAL, u % 2, 2, u % 2)
    k = (u - ALONE) // 2
    if u % 2 == 0:
        return Step(u, "A", LAG + k, 0, 1, k % 2)
    return Step(u, "B", k, 1, 1, k % 2)


def later(step, it):
    rate = ROUND // 2 if step.part == 1 else ROUND
    return Step(step.n + it * ROUND, step.stream, step.strip + it * rate, step.parity, step.part, step.odd)


def walk(eng, body):
    for lo, hi, looped in SCHEDULE:
        if looped:
            with eng.Fori(0, (hi - lo) // ROUND) as it:
                for u in range(lo, lo + ROUND):
                    body(*[later(step_at(u + k), it) for k in (-2, -1, 0, 1, 2)])
        else:
            for u in range(lo, hi):
                body(*[step_at(u + k) for k in (-2, -1, 0, 1, 2)])


def at_least(eng, sem, value):
    if not isinstance(value, int) or value > 0:
        eng.wait_ge(sem, value)


def when(eng, value, wanted, body):
    if isinstance(value, int):
        if value == wanted:
            body()
    else:
        with eng.If(value == wanted):
            body()


def ring_at(eng, strip):
    r = strip % (RING * STRIPS)
    gap = IMG - STRIPS * ROWS_STRIP
    if isinstance(strip, int):
        return r * ROWS_STRIP + (r // STRIPS) * gap
    r = eng.snap(r)
    return eng.snap(r * ROWS_STRIP + (r >> 3) * gap).with_bounds(min_val=0, max_val=RING * IMG - gap - ROWS_STRIP)


def rows(ring, off, col, width=SIDE, n=WS):
    v = ring[:, bass.ds(off + col, (n - 1) * PITCH + width)]
    return bass.AP(v.tensor, v.offset, [v.ap[0], [PITCH, n], [1, width]])


CHAN, MEAN, VAR = 0, 1, 5


def at_phase(eng, step, phases, body, first_x=0, order="AB"):
    if step is None or not step.leads:
        return
    phases = [p for p in phases if p % 2 == step.odd]
    if not phases:
        return
    g = step.g
    x_image, x1_image = (g >> 3) + 1, (g >> 3) - 1

    def both(phase):
        for s in order:
            body(phase, s, x_image if s == "A" else x1_image)
    if isinstance(g, int):
        if g % STRIPS in phases:
            for s in order:
                if s == "A" and first_x <= g < TOTAL:
                    body(g % STRIPS, "A", x_image)
                if s == "B" and STRIPS <= g < TOTAL + STRIPS:
                    body(g % STRIPS, "B", x1_image)
    elif step.part == 1 and len(phases) == 1:
        when(eng, g & (STRIPS - 1), phases[0], lambda: both(phases[0]))
    elif step.part == 1:
        when(eng, g & 3, MEAN & 3, lambda: [when(eng, g & (STRIPS - 1), p, lambda: both(p)) for p in phases])
    else:
        for p in phases:
            if step.part == 0:
                when(eng, g, p, lambda: body(p, "A", x_image))
                when(eng, g, p + STRIPS, lambda: both(p))
            else:
                when(eng, g, p + TOTAL, lambda: body(p, "B", x1_image))


def window_attention_layers(nc, x, qkv_w, qkv_b, proj_w, proj_b, bias_rev, mask, ident_in, group_in, out):
    with ExitStack() as ctx:
        ctx.enter_context(nc.allow_non_contiguous_dma("small loads of biases and the relative bias table"))

        def sb(name, shape, dtype=F32):
            return ctx.enter_context(nc.sbuf_tensor(name, shape, dtype))

        def sem(name):
            return ctx.enter_context(nc.semaphore(name))

        low_banks = ctx.enter_context(nc.psum_tensor("low_banks", [128, 4, 512], F32))
        pt_banks = low_banks[:, 0:2, :]
        swap_bank = low_banks[:, 2, :]
        score_bank = (0, 3)
        q_bank, k_bank = [ctx.enter_context(nc.psum_tensor(f"{b}_bank", [128, 512], F32)) for b in ("q", "k")]
        o_banks = ctx.enter_context(nc.psum_tensor("o_banks", [128, 2, 512], F32))
        y_bank = k_bank
        v_bank, ot_bank = o_banks[:, 0, :], o_banks[:, 1, :]
        o_groups = o_banks[:, :, 0:HEADS * 2 * VW].rearrange("p b (g v) -> p b g v", v=VW)
        stat_col = {"A": low_banks[:, 1, 508:509], "B": low_banks[:, 1, 509:510]}

        ident = sb("ident", [128, 128])
        group_avg = sb("group_avg", [128, 128])
        w_qkv = {s: sb(f"w_qkv_{s}", [CH, 3 * CH]) for s in "AB"}
        w_hi = {s: sb(f"w_hi_{s}", [CH, 2 * CH], F32R) for s in "AB"}
        w_lo = {s: sb(f"w_lo_{s}", [CH, 2 * CH], F32R) for s in "AB"}
        w_proj = {s: sb(f"w_proj_{s}", [CH, CH]) for s in "AB"}
        b_qkv = {s: sb(f"b_qkv_{s}", [CH, 3]) for s in "AB"}
        b_proj = {s: sb(f"b_proj_{s}", [CH, 1]) for s in "AB"}
        one_head = sb("one_head", [128, 2])
        b_k_pair = {s: sb(f"b_k_pair_{s}", [CH, 2]) for s in "AB"}
        b_q_scaled = {s: sb(f"b_q_scaled_{s}", [CH, 1]) for s in "AB"}
        mask_tab = sb("mask_tab", [128, 2 * PAIRS * N])
        bias_tab = sb("bias_tab", [128, HEADS * N])
        minus_half = sb("minus_half", [128, 1])
        eps = sb("eps", [128, 1])
        idle_dve = {s: sb(f"idle_dve_{s}", [128, 1]) for s in "AB"}
        idle_after = {s: sb(f"idle_after_{s}", [128, 1]) for s in "AB"}
        zero = sb("zero", [128, 1])

        xr = sb("xr", [128, RING * IMG])
        x1r = sb("x1r", [128, RING * IMG])
        x_in = [sb(f"x_in{i}", [PT, JT * CH]) for i in range(2)]
        xn = [sb(f"xn{i}", [128, WINS * WPAD]) for i in range(2)]
        xn_hi = sb("xn_hi", [128, TOK], F32R)
        xn_lo = sb("xn_lo", [128, TOK], F32R)
        q_t = sb("q_t", [128, TOK])
        k_pair = sb("k_pair", [128, WINS, 2, N])
        v_bd = [sb(f"v_bd{i}", [128, 2, 2, HEADS, 2, VW]) for i in range(2)]
        logits = sb("logits", [128, 2, PAIRS, 2, N])
        neg_max = sb("neg_max", [128, 2, PAIRS, 2])
        probs = sb("probs", [128, HEADS, PAIRS, WPAD])
        probs_t = sb("probs_t", [128, 2, 2, 2, 2, N])
        sums = sb("sums", [128, 2, HEADS * 2])
        inv_sums = sb("inv_sums", [128, 2, HEADS * 2])
        o_sb = sb("o_sb", [128, PAIRS, CH])
        o_t = sb("o_t", [128, TOK])
        y_t = sb("y_t", [128, TOK])
        out_st = sb("out_st", [PT, JT * CH])
        bn = {s: sb(f"bn_{s}", [128, STRIPS * 6]) for s in "AB"}
        chan = {s: sb(f"chan_{s}", [128, 2]) for s in "AB"}
        gmean = {s: sb(f"gmean_{s}", [128, 1]) for s in "AB"}
        dev = {s: sb(f"dev_{s}", [128, 1]) for s in "AB"}
        dev2 = {s: sb(f"dev2_{s}", [128, 1]) for s in "AB"}
        spread = {s: sb(f"spread_{s}", [128, 1]) for s in "AB"}
        gvar = {s: sb(f"gvar_{s}", [128, 1]) for s in "AB"}
        grstd = {s: sb(f"grstd_{s}", [128, 1]) for s in "AB"}
        cur_mean = {s: sb(f"cur_mean_{s}", [128, 1]) for s in "AB"}
        cur_rstd = {s: sb(f"cur_rstd_{s}", [128, 1]) for s in "AB"}

        consts_in = sem("consts_in")
        bias_in = sem("bias_in")
        buffers_set = sem("buffers_set")
        banks_set = sem("banks_set")
        head_flags = sem("head_flags")
        x_loaded = [sem(f"x_loaded{i}") for i in range(2)]
        x_swapped = sem("x_swapped")
        x_stored = sem("x_stored")
        x_padded = sem("x_padded")
        x1_padded = sem("x1_padded")
        norm_done = sem("norm_done")
        hi_done, lo_done = sem("hi_done"), sem("lo_done")
        w_split = sem("w_split")
        q_done, k_done, v_done = sem("q_done"), sem("k_done"), sem("v_done")
        q_copied, k_copied = sem("q_copied"), sem("k_copied")
        v_copied0, v_copied1 = sem("v_copied0"), sem("v_copied1")
        scores_done = sem("scores_done")
        biased = sem("biased")
        max_done = sem("max_done")
        shifted = sem("shifted")
        exp_done = sem("exp_done")
        pt_done, pt_copied = sem("pt_done"), sem("pt_copied")
        o_done = sem("o_done")
        sums_safe, sums_inverted = sem("sums_safe"), sem("sums_inverted")
        o_scaled = sem("o_scaled")
        ot_done, ot_copied = sem("ot_done"), sem("ot_copied")
        y_done, y_taken = sem("y_done"), sem("y_taken")
        x1_written = sem("x1_written")
        y_swapped, y_staged, y_stored = sem("y_swapped"), sem("y_staged"), sem("y_stored")
        bn_done = {s: sem(f"bn_done_{s}") for s in "AB"}
        chan_done = {s: sem(f"chan_done_{s}") for s in "AB"}
        gmean_mm = {s: sem(f"gmean_mm_{s}") for s in "AB"}
        gmean_out = {s: sem(f"gmean_out_{s}") for s in "AB"}
        spread_out = {s: sem(f"spread_out_{s}") for s in "AB"}
        gvar_mm = {s: sem(f"gvar_mm_{s}") for s in "AB"}
        gvar_out = {s: sem(f"gvar_out_{s}") for s in "AB"}
        pool_step = sem("pool_step")
        stats_cur = {s: sem(f"stats_cur_{s}") for s in "AB"}

        def stat_matmul(pe, s, image):
            at_least(pe, chan_done[s], image + 1)
            nc.tensor.matmul(stat_col[s], group_avg[:, :], chan[s][:, 0:1], start=True, stop=True)\
                .then_inc(gmean_mm[s], 1)

        def spread_matmul(pe, s, image):
            at_least(pe, spread_out[s], image + 1)
            nc.tensor.matmul(stat_col[s], group_avg[:, :], spread[s][:, :], start=True, stop=True)\
                .then_inc(gvar_mm[s], 1)

        def mean_copy(act, s, image):
            at_least(act, gmean_mm[s], image + 1)
            nc.scalar.copy(gmean[s][:, :], stat_col[s]).then_inc(gmean_out[s], 1)

        def var_copy(act, s, image):
            at_least(act, gvar_mm[s], image + 1)
            nc.scalar.activation(gvar[s][:, :], stat_col[s], ACT.Identity, bias=eps[:, :]).then_inc(gvar_out[s], 1)

        def windows_of(tokens):
            return tokens[:, :].rearrange("p (w q) -> p w q", q=WPAD)[:, :, 0:N]

        def stat_copy(act):
            return lambda phase, s, image: (mean_copy if phase == MEAN else var_copy)(act, s, image)

        def stat_product(pe, cur):
            def product(phase, s, image):
                at_least(pe, pt_copied, cur.n * 2 + 1)
                (stat_matmul if phase == MEAN else spread_matmul)(pe, s, image)
            return product

        def v_half(step, a):
            src = o_banks[a * WPAD:(a + 1) * WPAD, 0, :].rearrange("p (g h d) -> p g h d", g=4, h=HEADS)
            dst = v_bd[step.parity][a * WPAD:(a + 1) * WPAD].rearrange("p b w h a v -> p (b w) h a v")
            return dst[:, :, :, a, 0:HD], src

        block = ctx.enter_context(nc.Block())

        @block.sync
        def _(sp):
            def chunk(images, k):
                at = k * (TOK * CH)
                return bass.AP(images.tensor, at if isinstance(k, int) else sp.snap(at),
                               [[JT * CH, PT], [1, JT * CH]])

            def load(c, k, slot, swapped):
                src = chunk(x, k)
                if not isinstance(swapped, int):
                    swapped = sp.snap(swapped)
                at_least(sp, x_swapped, swapped)
                sp.dma_start(x_in[slot][:, :], src).then_inc(x_loaded[slot], 16)

            for slot in range(2):
                load(slot, slot, slot, 0)
            sp.dma_start(ident[:, :], ident_in).then_inc(consts_in, 16)
            sp.dma_start(group_avg[:, :], group_in).then_inc(consts_in, 16)
            for s in "AB":
                sp.dma_start(w_qkv[s][:, :], qkv_w[s]).then_inc(consts_in, 16)
                sp.dma_start(w_proj[s][:, :], proj_w[s]).then_inc(consts_in, 16)
                sp.dma_start(b_qkv[s][:, :], qkv_b[s].rearrange("(t p) -> p t", p=CH)).then_inc(consts_in, 16)
                sp.dma_start(b_proj[s][:, :], proj_b[s].rearrange("(p o) -> p o", o=1)).then_inc(consts_in, 16)
            sp.dma_start(mask_tab[:, :], mask).then_inc(consts_in, 16)
            def relative_bias(q):
                first = (WS - 1 - q // WS) * TABLE_SIDE + WS - 1 - q % WS
                src = bass.AP(bias_rev.tensor, bias_rev.offset + first,
                              [[TABLE_SIDE ** 2, 1], [TABLE_SIDE ** 2, HEADS], [TABLE_SIDE, WS], [1, WS]])
                dst = bias_tab[q:q + 1, :].rearrange("p (h a b) -> p h a b", h=HEADS, a=WS)
                sp.dma_start(dst, src).then_inc(bias_in, 16)

            for c in range(2, LEAD + 1):
                load(c, c, c % 2, c - 1)
                if c == 2:
                    sp.wait_ge(buffers_set, 1)
                for q in range((c - 2) * 4, min((c - 1) * 4, N)):
                    relative_bias(q)
            sp.wait_ge(bias_in, N * 16)
            sp.dma_start(bias_tab[WPAD:WPAD + N, :], bias_tab[0:N, :]).then_inc(bias_in, 16)

            def step(before, prev, cur, nxt, after):
                if cur is not None and cur.stream == "A":
                    c = cur.strip + LEAD + 1
                    if isinstance(c, int):
                        if c < TOTAL + LEAD:
                            paired = c < LAG + LEAD
                            load(c, c % TOTAL, c % 2 if paired else 0, c - 1 if paired else c)
                    elif cur.part == 0:
                        load(c, c, 1 - cur.parity, c - 1)
                    else:
                        load(c, c % TOTAL, 0, c)
                if before is not None and before.stream == "B":
                    m = before.strip
                    at_least(sp, y_staged, m + 1)
                    sp.dma_start(chunk(out, m), out_st[:, :]).then_inc(y_stored, 16)
            walk(sp, step)
            sp.wait_ge(y_stored, TOTAL * 16)

        @block.gpsimd
        def _(pool):
            nc.gpsimd.memset(zero[:, :], 0.0)
            nc.gpsimd.memset(minus_half[:, :], -0.5).then_inc(pool_step, 1)
            pool.wait_ge(pool_step, 1)

            def pad_image(ring, img, done, to_low):
                off = img % RING * IMG
                own = SHIFT if to_low else 0
                for r0, c0, n, width, dr, dc in ((own, 0, SIDE, SHIFT, 0, 1), (0, own, SHIFT, SIDE, 1, 0),
                                                 (0, 0, SHIFT, SHIFT, 1, 1)):
                    first = rows(ring, off + r0 * PITCH, c0, width, n)
                    second = rows(ring, off + (r0 + dr * SIDE) * PITCH, c0 + dc * SIDE, width, n)
                    dst, src = (first, second) if to_low else (second, first)
                    nc.gpsimd.tensor_copy(dst, src).then_inc(done, 1)

            def spread_of(s, img, before):
                pool.wait_ge(gmean_out[s], img + 1)
                nc.gpsimd.tensor_tensor(dev[s][:, :], chan[s][:, 0:1], gmean[s][:, :], ALU.subtract)\
                    .then_inc(pool_step, 1)
                pool.wait_ge(pool_step, before + 1)
                nc.gpsimd.tensor_tensor(dev2[s][:, :], dev[s][:, :], dev[s][:, :], ALU.mult)\
                    .then_inc(pool_step, 1)
                pool.wait_ge(pool_step, before + 2)
                nc.gpsimd.tensor_tensor(spread[s][:, :], dev2[s][:, :], chan[s][:, 1:2], ALU.add)\
                    .then_inc(spread_out[s], 1)

            def invert(s, img, before):
                pool.wait_ge(gvar_out[s], img + 1)
                nc.gpsimd.tensor_tensor(grstd[s][:, :], gvar[s][:, :], minus_half[:, :], ALU.pow)\
                    .then_inc(pool_step, 1)
                pool.wait_ge(pool_step, before + 1)

            def publish(s, normed):
                for to, of in ((cur_mean[s], gmean[s]), (cur_rstd[s], grstd[s])):
                    at_least(pool, norm_done, normed)
                    nc.gpsimd.tensor_tensor(to[:, :], of[:, :], zero[:, :], ALU.add).then_inc(stats_cur[s], 1)

            pool.wait_ge(x_stored, STRIPS)
            pad_image(xr, 0, x_padded, False)
            spread_of("A", 0, 1)
            invert("A", 0, 3)
            publish("A", 0)
            pool.wait_ge(x_stored, 2 * STRIPS)
            pad_image(xr, 1, x_padded, False)

            def image(i, before, a_normed, b_normed):
                if b_normed is None:
                    spread_of("A", i + 1, before)
                    invert("A", i + 1, before + 2)
                else:
                    pool.wait_ge(x1_written, i * STRIPS)
                    pad_image(x1r, i - 1, x1_padded, True)
                    spread_of("A", i + 1, before)
                    spread_of("B", i - 1, before + 2)
                    invert("A", i + 1, before + 4)
                    invert("B", i - 1, before + 5)
                publish("A", a_normed)
                if b_normed is not None:
                    publish("B", b_normed)
                pool.wait_ge(x_stored, (i + 3) * STRIPS)
                pad_image(xr, i + 2, x_padded, False)

            image(0, 4, STRIPS, None)
            image(1, 7, 2 * STRIPS, 0)
            with pool.Fori(2, IMAGES) as i:
                image(i, i * 6 + 1, i * 16 - 1, i * 16)
            pool.wait_ge(x1_written, TOTAL)
            pad_image(x1r, IMAGES - 1, x1_padded, True)
            spread_of("B", IMAGES - 1, IMAGES * 6 + 1)
            invert("B", IMAGES - 1, IMAGES * 6 + 3)
            publish("B", STEPS - STRIPS)

        @block.scalar
        def _(act):
            act.wait_ge(consts_in, 16 * 11)
            act.wait_ge(buffers_set, 2)
            act.wait_ge(banks_set, 1)

            def place_of(c):
                dst = rows(xr, ring_at(act, c), 0)
                return bass.AP(dst.tensor, dst.offset, [dst.ap[0], [PITCH, WS], [JT, SIDE // JT], [1, JT]])

            def store_chunk(c, dst):
                src = swap_bank[:, 0:TOK].rearrange("p (j r q) -> p r q j", j=JT, r=WS)
                at_least(act, x_swapped, c + 1)
                nc.scalar.copy(dst, src).then_inc(x_stored, 1)

            def exponentials(st, k):
                at_least(act, shifted, st.n * 2 + k + 1)
                hp = HP_ORDER[k]
                dst = probs[:, 2 * hp:2 * hp + 2].rearrange("p h j k -> p j h k")[:, :, :, 0:N]
                nc.scalar.activation(dst, logits[:, hp], ACT.Exp).then_inc(exp_done, 1)

            def copy_probs(st, k):
                hp = HP_ORDER[k]
                at_least(act, pt_done, st.n * 2 + k + 1)
                src = pt_banks[:, hp, :].rearrange("p (b q) -> p b q", q=WPAD)[:, :, 0:N]
                dst = probs_t[:, hp].rearrange("p a b w q -> p (a b w) q")
                nc.scalar.copy(dst, src).then_inc(pt_copied, 1)

            with act.Fori(0, STRIPS) as c:
                store_chunk(c, place_of(c))
            with act.Fori(STRIPS, LEAD) as c:
                when(act, c, STRIPS + MEAN, lambda: mean_copy(act, "A", 0))
                when(act, c, STRIPS + VAR, lambda: var_copy(act, "A", 0))
                store_chunk(c, place_of(c))

            def step(before, prev, cur, nxt, after):
                if cur is not None and cur.stream == "A":
                    chunk_place = place_of(cur.strip + LEAD)
                if nxt is not None:
                    s = nxt.stream
                    at_least(act, q_done, nxt.n + 1)
                    nc.scalar.activation(q_t[:, :], q_bank[:, 0:TOK], ACT.Identity,
                                         bias=b_q_scaled[s][:, :], scale=SCALE[s]).then_inc(q_copied, 1)
                    at_least(act, k_done, nxt.n + 1)
                    for odd in range(2):
                        nc.scalar.activation(
                            k_pair[:, :, odd, :], k_bank[:, 0:TOK].rearrange("p (w k) -> p w k", k=N),
                            ACT.Identity, bias=b_k_pair[s][:, odd:odd + 1],
                            scale=one_head[:, odd:odd + 1]).then_inc(k_copied, 1)
                if cur is not None:
                    exponentials(cur, 1)
                    copy_probs(cur, 0)
                if prev is not None:
                    at_least(act, ot_done, prev.n + 1)
                    src = ot_bank.rearrange("p (w q) -> p w q", q=WPAD)[:, :, 0:N]\
                        .rearrange("p w (i j) -> p w i j", j=WS)
                    dst = o_t[:, :].rearrange("p (i w j) -> p w i j", w=WINS, j=WS)
                    nc.scalar.activation(dst, src, ACT.Identity, bias=b_qkv[prev.stream][:, 2:3])\
                        .then_inc(ot_copied, 1)
                if cur is not None:
                    copy_probs(cur, 1)
                if nxt is not None:
                    at_least(act, v_done, nxt.n + 1)
                    nc.scalar.copy(*v_half(nxt, 0)).then_inc(v_copied0, 1)
                if after is not None:
                    at_least(act, norm_done, after.n + 1)
                    nc.scalar.copy(xn_hi[:, :].rearrange("p (w q) -> p w q", q=N), windows_of(xn[after.parity]))\
                        .then_inc(hi_done, 1)
                if cur is not None and cur.stream == "A":
                    store_chunk(cur.strip + LEAD, chunk_place)
                if before is not None and before.stream == "B":
                    m = before.strip
                    at_least(act, y_stored, m * 16)
                    at_least(act, y_swapped, m + 1)
                    nc.scalar.copy(out_st[:, :], low_banks[0:PT, 2, :]).then_inc(y_staged, 1)
                at_phase(act, cur, (MEAN, VAR), stat_copy(act), order="BA")
                if nxt is not None:
                    exponentials(nxt, 0)
            walk(act, step)

        @block.vector
        def _(dve):
            for buf in (bias_tab, probs, xn[0], xn[1], v_bd[0]):
                shape = " ".join("abcdefg"[:len(buf.shape) - 1])
                nc.vector.memset(buf[:].rearrange(f"p {shape} -> p ({shape})"), 0.0)
            nc.vector.memset(v_bd[1][:].rearrange("p a b c d e -> p (a b c d e)"), 0.0).then_inc(buffers_set, 1)
            dve.wait_ge(buffers_set, 1)
            nc.vector.memset(eps[:, :], GN_EPS)
            for h in range(HEADS):
                for odd in range(2):
                    flag = nc.vector.memset(one_head[h * HD:(h + 1) * HD, odd:odd + 1], float(h % 2 == odd))
            flag.then_inc(head_flags, 1)
            dve.wait_ge(head_flags, 1)
            for i in range(2):
                for a in range(2):
                    ones = v_bd[i][a * WPAD:(a + 1) * WPAD].rearrange("p b w h a v -> p (b w h) a v")
                    nc.vector.memset(ones[:, :, a, HD:VW], 1.0)
            dve.wait_ge(consts_in, 16 * 11)
            for s in "AB":
                nc.vector.tensor_copy(w_hi[s][:, :], w_qkv[s][:, 0:2 * CH]).then_inc(w_split, 1)
            dve.wait_ge(w_split, 2)
            for s in "AB":
                nc.vector.tensor_tensor(w_lo[s][:, :], w_qkv[s][:, 0:2 * CH], w_hi[s][:, :].bitcast(F32),
                                        ALU.subtract)
            for s in "AB":
                nc.vector.tensor_scalar(b_k_pair[s][:, :], one_head[:, :], b_qkv[s][:, 1:2], None, ALU.mult)
            nc.vector.tensor_scalar(b_q_scaled["A"][:, :], b_qkv["A"][:, 0:1], SCALE["A"], None, ALU.mult)
            nc.vector.tensor_scalar(b_q_scaled["B"][:, :], b_qkv["B"][:, 0:1], SCALE["B"], None, ALU.mult)\
                .then_inc(buffers_set, 1)
            for b in (q_bank[:, :], k_bank[:, :], v_bank, ot_bank):
                nc.vector.memset(b, 0.0)
            nc.vector.memset(low_banks[:, :, :].rearrange("p h c -> p (h c)"), 0.0).then_inc(banks_set, 1)

            def chunk_stats(c):
                at_least(dve, x_stored, c + 1)
                nc.vector.bn_stats(bn["A"][:, bass.ds((c & 7) * 6, 6)], rows(xr, ring_at(dve, c), 0))\
                    .then_inc(bn_done["A"], 1)

            def channel_stats(s, count, done):
                at_least(dve, bn_done[s] if s == "A" else x1_written, count)
                nc.vector.memset(idle_dve[s][:, :], 0.0)
                nc.vector.bn_aggr(chan[s][:, :], bn[s][:, :]).then_inc(chan_done[s], 1)
                at_least(dve, chan_done[s], done)
                nc.vector.memset(idle_after[s][:, :], 0.0)

            for first in (0, STRIPS):
                with dve.Fori(first, first + STRIPS) as c:
                    chunk_stats(c)
                if first == 0:
                    channel_stats("A", STRIPS, 1)
            dve.wait_ge(stats_cur["A"], 2)
            channel_stats("A", 2 * STRIPS, 2)

            def normalise(st):
                s, strip = st.stream, st.strip
                at_least(dve, v_done, st.n - 1)
                img = strip >> 3
                at_least(dve, stats_cur[s], img * 2 + 2)
                at_least(dve, x_padded if s == "A" else x1_padded, img * 3 + 3)
                off = ring_at(dve, strip)
                start = SHIFT * PITCH + SHIFT if s == "A" else 0
                v = rows(xr if s == "A" else x1r, off + start, 0)
                src = bass.AP(v.tensor, v.offset, [v.ap[0], [WS, WINS], [PITCH, WS], [1, WS]])
                dst = xn[st.parity][:, :].rearrange("p (w q) -> p w q", q=WPAD)[:, :, 0:N]\
                    .rearrange("p w (i j) -> p w i j", j=WS)
                nc.vector.tensor_scalar(dst, src, cur_mean[s][:, :], cur_rstd[s][:, :],
                                        ALU.subtract, ALU.mult).then_inc(norm_done, 1)

            def low_part(st):
                at_least(dve, hi_done, st.n + 1)
                nc.vector.tensor_tensor(
                    xn_lo[:, :].rearrange("p (w q) -> p w q", q=N), windows_of(xn[st.parity]),
                    xn_hi[:, :].bitcast(F32).rearrange("p (w q) -> p w q", q=N), ALU.subtract)\
                    .then_inc(lo_done, 1)

            def add_table(st, k):
                hp = HP_ORDER[k]
                n = st.n * 2 + k + 1
                if st.stream == "A":
                    last = (st.strip & 7) + 1 >> 3
                    table = mask_tab[:, bass.ds(last * (PAIRS * N), PAIRS * N)]
                    table = bass.AP(table.tensor, table.offset, [table.ap[0], [N, PAIRS], [0, 2], [1, N]])
                else:
                    if k == 0:
                        at_least(dve, bias_in, (N + 1) * 16)
                    table = bias_tab[:, 2 * hp * N:(2 * hp + 2) * N]
                    table = bass.AP(table.tensor, table.offset, [table.ap[0], [0, PAIRS], [N, 2], [1, N]])
                at_least(dve, scores_done, n)
                nc.vector.tensor_tensor(
                    logits[:, hp],
                    low_banks[:, score_bank[hp], 0:PAIRS * 2 * N].rearrange("p (j h k) -> p j h k", h=2, k=N),
                    table, ALU.add).then_inc(biased, 1)

            def row_max(st, k):
                hp = HP_ORDER[k]
                at_least(dve, biased, st.n * 2 + k + 1)
                nc.vector.tensor_reduce(neg_max[:, hp], logits[:, hp], AX.X, ALU.max, negate=True)\
                    .then_inc(max_done, 1)

            def subtract_max(st, k):
                hp = HP_ORDER[k]
                at_least(dve, max_done, st.n * 2 + k + 1)
                top = neg_max[:, hp]
                top = bass.AP(top.tensor, top.offset, [top.ap[0], [2, PAIRS], [1, 2], [0, N]])
                nc.vector.tensor_tensor(logits[:, hp], logits[:, hp], top, ALU.add).then_inc(shifted, 1)

            def add_residual(st):
                s = st.stream
                off = ring_at(dve, st.strip)
                at_least(dve, y_done, st.n + 1)
                y = y_bank[:, 0:TOK].rearrange("p (i c) -> p i c", i=WS)
                if s == "A":
                    place = off + SHIFT * PITCH
                    nc.vector.scalar_tensor_tensor(
                        rows(x1r, place, SHIFT), y, b_proj[s][:, :], rows(xr, place, SHIFT),
                        ALU.add, ALU.add).then_inc(y_taken, 1)
                else:
                    nc.vector.scalar_tensor_tensor(
                        y_t[:, :].rearrange("p (i c) -> p i c", i=WS), y, b_proj[s][:, :],
                        rows(x1r, off, 0), ALU.add, ALU.add).then_inc(y_taken, 1)

            def x1_stats(st):
                at_least(dve, y_taken, st.n + 1)
                nc.vector.bn_stats(bn["B"][:, bass.ds((st.strip & 7) * 6, 6)],
                                   rows(x1r, ring_at(dve, st.strip) + SHIFT * PITCH, SHIFT)).then_inc(x1_written, 1)

            def clamp_sums(st):
                at_least(dve, o_done, st.n + 1)
                nc.vector.tensor_scalar(sums[:, :, :], o_groups[:, :, :, HD], 0.5, None, ALU.max)\
                    .then_inc(sums_safe, 1)

            def invert_sums(st):
                at_least(dve, sums_safe, st.n + 1)
                nc.vector.reciprocal(inv_sums[:, :, :], sums[:, :, :]).then_inc(sums_inverted, 1)

            def scale_outputs(st, pp):
                at_least(dve, sums_inverted, st.n + 1)
                inv = inv_sums[:, pp]
                inv = bass.AP(inv.tensor, inv.offset, [inv.ap[0], [1, 2 * HEADS], [0, HD]])
                nc.vector.tensor_tensor(
                    o_sb[:, 2 * pp:2 * pp + 2, :].rearrange("p a (h d) -> p (a h) d", h=HEADS),
                    o_groups[:, pp, :, 0:HD], inv, ALU.mult).then_inc(o_scaled, 1)

            def step(before, prev, cur, nxt, after):
                if nxt is not None:
                    at_least(dve, v_done, nxt.n + 1)
                    nc.vector.tensor_copy(*v_half(nxt, 1)).then_inc(v_copied1, 1)
                chunk = cur.strip + LEAD if cur is not None and cur.stream == "A" else None
                if before is not None and before.stream == "A" and prev.stream == "B":
                    x1_stats(before)
                if after is not None:
                    normalise(after)
                if nxt is not None:
                    add_table(nxt, 0)
                    row_max(nxt, 0)
                if after is not None:
                    low_part(after)
                if nxt is not None:
                    subtract_max(nxt, 0)
                if prev is not None:
                    add_residual(prev)
                if cur is not None:
                    clamp_sums(cur)
                if prev is not None and prev.stream == "A" and cur.stream == "A":
                    x1_stats(prev)
                if cur is not None:
                    invert_sums(cur)
                if nxt is not None:
                    add_table(nxt, 1)
                if cur is not None:
                    scale_outputs(cur, 0)
                at_phase(dve, cur, (CHAN,), lambda phase, s, image: channel_stats(
                    s, (image + 1) * STRIPS, image + 1), first_x=STRIPS)
                if nxt is not None:
                    row_max(nxt, 1)
                if cur is not None:
                    scale_outputs(cur, 1)
                if nxt is not None:
                    subtract_max(nxt, 1)
                if chunk is not None:
                    chunk_stats(chunk)

            walk(dve, step)

        @block.tensor
        def _(pe):
            pe.wait_ge(consts_in, 16 * 11)
            pe.wait_ge(banks_set, 1)
            pe.wait_ge(buffers_set, 2)

            def swap_chunk(c, slot, loaded):
                at_least(pe, x_loaded[slot], loaded)
                for j in range(JT):
                    last = nc.tensor.transpose(swap_bank[:, j * PT:(j + 1) * PT],
                                               x_in[slot][:, j * CH:(j + 1) * CH], ident[0:PT, 0:PT])
                last.then_inc(x_swapped, 1)

            def first_chunks(half_c):
                for slot in range(2):
                    c = half_c * 2 + slot
                    at_least(pe, x_stored, c)
                    if not isinstance(c, int):
                        when(pe, c, STRIPS + MEAN, lambda: stat_matmul(pe, "A", 0))
                        when(pe, c, STRIPS + VAR, lambda: spread_matmul(pe, "A", 0))
                    swap_chunk(c, slot, half_c * 16 + 16)

            first_chunks(0)
            with pe.Fori(1, LEAD // 2) as half_c:
                first_chunks(half_c)
            pe.wait_ge(x_stored, LEAD)

            def project(bank, s, part):
                cols = slice(part * CH, (part + 1) * CH)
                products = ((w_hi[s], xn_hi), (w_lo[s], xn_hi), (w_hi[s], xn_lo))
                for i, (w, tokens) in enumerate(products):
                    last = nc.tensor.matmul(bank[:, 0:TOK], w[:, cols], tokens[:, :], start=i == 0,
                                            stop=i == len(products) - 1)
                return last

            def scores(hp):
                channels = slice(2 * hp * HD, (2 * hp + 2) * HD)
                for win in range(WINS):
                    j, half = place(win)
                    last = nc.tensor.matmul(
                        low_banks[half * WPAD:half * WPAD + N, score_bank[hp], j * 2 * N:(j + 1) * 2 * N],
                        q_t[channels, win * N:(win + 1) * N],
                        k_pair[channels, win].rearrange("p h k -> p (h k)"), start=True, stop=True)
                last.then_inc(scores_done, 1)

            def transpose_probs(st, k):
                hp = HP_ORDER[k]
                at_least(pe, exp_done, st.n * 2 + k + 1)
                for h2 in range(2):
                    for pp in range(2):
                        b = h2 * 2 + pp
                        last = nc.tensor.transpose(
                            pt_banks[:, hp, b * 128:(b + 1) * 128],
                            probs[:, 2 * hp + h2, 2 * pp:2 * pp + 2, :].rearrange("p j k -> p (j k)"),
                            ident[:, :])
                last.then_inc(pt_done, 1)

            def step(before, prev, cur, nxt, after):
                if nxt is not None:
                    w, tokens = w_qkv[nxt.stream], xn[nxt.parity]
                    at_least(pe, lo_done, nxt.n + 1)
                    at_least(pe, q_copied, nxt.n)
                    project(q_bank, nxt.stream, 0).then_inc(q_done, 1)
                    at_least(pe, y_taken, nxt.n - 2)
                    project(k_bank, nxt.stream, 1).then_inc(k_done, 1)
                if cur is not None and cur.stream == "A":
                    c = cur.strip + LEAD
                    if cur.part == 0:
                        slot = cur.parity
                        loaded = ((c >> 1) + 1) * 16
                    else:
                        slot = 0
                        loaded = (c - (LAG + LEAD) // 2 + 1) * 16
                    at_least(pe, x_stored, c)
                    if prev is not None and prev.stream == "B":
                        at_least(pe, y_staged, prev.strip)
                    swap_chunk(c, slot, loaded)
                if before is not None and before.stream == "B":
                    if prev is not None and prev.stream == "A":
                        at_least(pe, x_stored, prev.strip + LEAD + 1)
                    else:
                        at_least(pe, y_staged, before.strip)
                    at_least(pe, y_taken, before.n + 1)
                    for j in range(JT):
                        last = nc.tensor.transpose(low_banks[0:PT, 2, j * CH:(j + 1) * CH],
                                                   y_t[:, j::JT], ident[:, :])
                    last.then_inc(y_swapped, 1)
                if nxt is not None:
                    at_least(pe, o_scaled, nxt.n * 2 - 3)
                    if prev is None:
                        at_least(pe, v_copied0, nxt.n)
                        at_least(pe, v_copied1, nxt.n)
                    for b in range(WINS // 2):
                        last = nc.tensor.matmul(o_banks[:, 0, b * CH:(b + 1) * CH],
                                                tokens[:, b * 2 * WPAD:(b + 1) * 2 * WPAD],
                                                w[:, 2 * CH:3 * CH], start=True, stop=True)
                    last.then_inc(v_done, 1)
                if cur is not None:
                    transpose_probs(cur, 0)
                if prev is not None:
                    at_least(pe, o_scaled, prev.n * 2 + 2)
                    for j in range(PAIRS):
                        first = (4 * (j // 2) + j % 2) * WPAD
                        dst = o_banks[:, 1, first:first + 3 * WPAD]
                        dst = bass.AP(dst.tensor, dst.offset, [dst.ap[0], [2 * WPAD, 2], [1, WPAD]])
                        last = nc.tensor.transpose(dst, o_sb[:, j, :], ident[:, :])
                    last.then_inc(ot_done, 1)
                if cur is not None:
                    transpose_probs(cur, 1)
                if nxt is not None:
                    if cur is None:
                        at_least(pe, q_copied, nxt.n + 1)
                        at_least(pe, k_copied, nxt.n * 2 + 2)
                    scores(HP_ORDER[0])
                at_phase(pe, cur, (MEAN, VAR), stat_product(pe, cur))
                if prev is not None:
                    at_least(pe, ot_copied, prev.n + 1)
                    nc.tensor.matmul(y_bank[:, 0:TOK], w_proj[prev.stream][:, :], o_t[:, :],
                                     start=True, stop=True).then_inc(y_done, 1)
                if cur is not None:
                    at_least(pe, pt_copied, cur.n * 2 + 2)
                    if nxt is not None:
                        at_least(pe, v_copied0, nxt.n + 1)
                        at_least(pe, v_copied1, nxt.n + 1)
                    for pp in range(2):
                        for h in range(HEADS):
                            for half in range(2):
                                of_pairs = o_groups[half * WPAD:half * WPAD + N, pp, h::HEADS, :]
                                last = nc.tensor.matmul(
                                    of_pairs, probs_t[:, h // 2, h % 2, pp, half, :],
                                    v_bd[cur.parity][:, pp, half, h].rearrange("p a v -> p (a v)"),
                                    start=True, stop=True)
                    last.then_inc(o_done, 1)
                if nxt is not None:
                    scores(HP_ORDER[1])
            walk(pe, step)


def kernel(x, L0_conv_qkv_w, L0_conv_qkv_b, L0_conv_proj_w, L0_conv_proj_b,
           L1_conv_qkv_w, L1_conv_qkv_b, L1_conv_proj_w, L1_conv_proj_b, L1_conv_bias_table):
    import numpy as np
    import concourse.bacc as bacc
    from concourse.bass_utils import run_bass_kernel_spmd

    region = np.zeros((SIDE, SIDE), np.int32)
    cuts = (slice(0, -WS), slice(-WS, -SHIFT), slice(-SHIFT, None))
    for a, rs in enumerate(cuts):
        for b, cs in enumerate(cuts):
            region[rs, cs] = 3 * a + b
    mask = np.zeros((128, 2, PAIRS, N), np.float32)
    for last in range(2):
        for win in range(WINS):
            r = region[(STRIPS - 1) * last * WS:((STRIPS - 1) * last + 1) * WS,
                       win * WS:(win + 1) * WS].reshape(-1)
            pair, half = place(win)
            q = half * WPAD
            mask[q:q + N, last, pair] = np.where(r[:, None] != r[None, :], -1e9, 0.0)

    feeds = {
        "x": x, "mask": mask.reshape(128, -1), "ident": np.eye(128, dtype=np.float32),
        "group": np.kron(np.eye(GROUPS), np.full((CH // GROUPS,) * 2, GROUPS / CH)).astype(np.float32),
        "bias_rev": np.ascontiguousarray(np.asarray(L1_conv_bias_table)[::-1].T),
        "qkv_w_A": L0_conv_qkv_w, "qkv_b_A": L0_conv_qkv_b, "proj_w_A": L0_conv_proj_w, "proj_b_A": L0_conv_proj_b,
        "qkv_w_B": L1_conv_qkv_w, "qkv_b_B": L1_conv_qkv_b, "proj_w_B": L1_conv_proj_w, "proj_b_B": L1_conv_proj_b,
    }
    feeds = {k: np.ascontiguousarray(v) for k, v in feeds.items()}
    nc = bacc.Bacc("TRN2", target_bir_lowering=False, num_devices=1)
    d = {k: nc.dram_tensor(f"in_{k}", v.shape, mybir.dt.from_np(v.dtype), kind="ExternalInput").ap()
         for k, v in feeds.items()}
    out = nc.dram_tensor("out", feeds["x"].shape, F32, kind="ExternalOutput").ap()
    window_attention_layers(
        nc, d["x"], {s: d[f"qkv_w_{s}"] for s in "AB"}, {s: d[f"qkv_b_{s}"] for s in "AB"},
        {s: d[f"proj_w_{s}"] for s in "AB"}, {s: d[f"proj_b_{s}"] for s in "AB"},
        d["bias_rev"], d["mask"], d["ident"], d["group"], out)
    r = run_bass_kernel_spmd(nc, [{f"in_{k}": v for k, v in feeds.items()}], core_ids=[0])
    return r.results[0]["out"]
```
